# Optimizing a Trainium2 kernel written in Bass

```python
import numpy as np
import jax
import jax.numpy as jnp

def _softmax(x, axis=-1):
    return jax.nn.softmax(x, axis=axis)

def _gelu(x):
    return jax.nn.gelu(x, approximate=True)

def _silu(x):
    return jax.nn.silu(x)

def _sigmoid(x):
    return jax.nn.sigmoid(x)

def _layernorm(x, axis=-1, eps=1e-05):
    m = jnp.mean(x, axis=axis, keepdims=True)
    v = jnp.var(x, axis=axis, keepdims=True)
    return (x - m) / jnp.sqrt(v + eps)

def _scatter_add(tgt, idx, src, axis=0):
    return tgt.at[idx].add(src)

def _segment_sum(src, seg, n):
    return jax.ops.segment_sum(src, seg, n)
kernel_name = 'mk_xattn_ffn_d1_seqx_r8_2634f3'

def setup_inputs(seed: int=0):
    np.random.seed(seed)
    _w = jnp.asarray

    def _rec_inputs():
        import jax
        import jax.numpy as jnp
        _rk = jax.random.key(seed)
        x = 7.22e-05 + 1 * jax.random.normal(jax.random.fold_in(_rk, 1), (32, 56, 256), jnp.float32)
        _lenS = 56 - jax.random.randint(jax.random.fold_in(_rk, 7), (32,), 0, max(1, 56 // 4) + 1, jnp.int32)
        _lenS2 = 1500 - jax.random.randint(jax.random.fold_in(_rk, 8), (32,), 0, max(1, 1500 // 4) + 1, jnp.int32)
        _ctx_2048P = jax.random.normal(jax.random.fold_in(_rk, 11), (32, 16, 256), jnp.float32)
        _ctx_2048c = jax.random.dirichlet(jax.random.fold_in(_rk, 511), 0.3 * jnp.ones((16,), jnp.float32), (32, 1500))
        _ctx_2048t = jnp.einsum('bsk,bkd->bsd', _ctx_2048c, _ctx_2048P)
        _ctx_2048t = _ctx_2048t * jax.lax.rsqrt(jnp.mean(jnp.square(_ctx_2048t)) + 1e-12) * 0.953939
        ctx_2048 = 4.13588e-05 + 0.999923 * (_ctx_2048t + 0.3 * jax.random.normal(jax.random.fold_in(_rk, 611), (32, 1500, 256), jnp.float32))
        _validS = jnp.arange(56)[None, :] < _lenS[:, None]
        _validS2 = jnp.arange(1500)[None, :] < _lenS2[:, None]
        _causal = jnp.tril(jnp.ones((56, 56), dtype=bool))
        mask_BxS2_bf1 = jnp.ones((32, 1500), dtype=bool)
        return (x, ctx_2048, mask_BxS2_bf1)
    x, ctx_2048, mask_BxS2_bf1 = _rec_inputs()

    def _L0_xattn_setup():
        import jax, jax.numpy as jnp
        import numpy as np
        import math
        D_MODEL = 256
        N_Q_HEADS = 16
        N_KV_HEADS = 4
        HEAD_DIM = D_MODEL // N_Q_HEADS
        B = 4
        S = 128

        def _alibi_slopes(num_heads):
            n = 2 ** int(math.floor(math.log2(num_heads)))
            m0 = 2.0 ** (-8.0 / n)
            return m0 ** jnp.arange(1, n + 1, dtype=jnp.float32)
        key = jax.random.key(seed)
        ks = jax.random.split(key, 8)
        xavier = lambda k, fi, fo: jax.random.normal(k, (fi, fo), jnp.float32) * math.sqrt(2.0 / (fi + fo))
        return {'query': jax.random.normal(ks[0], (B, S, D_MODEL), jnp.float32), 'key': jax.random.normal(ks[1], (B, S, D_MODEL), jnp.float32), 'value': jax.random.normal(ks[2], (B, S, D_MODEL), jnp.float32), 'mask': jnp.ones((B, S), dtype=bool), 'Wq': xavier(ks[3], D_MODEL, N_Q_HEADS * HEAD_DIM), 'Wk': xavier(ks[4], D_MODEL, N_KV_HEADS * HEAD_DIM), 'Wv': xavier(ks[5], D_MODEL, N_KV_HEADS * HEAD_DIM), 'Wo': xavier(ks[6], D_MODEL, D_MODEL)}
    _L0_xattn_all = _L0_xattn_setup()
    _L0_xattn_in = {k: v for k, v in _L0_xattn_all.items() if k in ('Wq', 'Wk', 'Wv', 'Wo')}
    del _L0_xattn_all

    def _L0_ffn_setup():
        import jax, jax.numpy as jnp
        import numpy as np
        HID = 256
        N_EXP = 32
        F_EXP = 96
        TOP_K = 6
        F_SH = 192
        B, S = (1, 128)
        key = jax.random.key(seed)
        ks = jax.random.split(key, 8)
        s = 0.02
        return {'hidden_states': jax.random.normal(ks[0], (B, S, HID), dtype=jnp.float32), 'gate_w': jax.random.normal(ks[1], (HID, N_EXP), dtype=jnp.float32) * s, 'wg': jax.random.normal(ks[2], (N_EXP, HID, F_EXP), dtype=jnp.float32) * s, 'wu': jax.random.normal(ks[3], (N_EXP, HID, F_EXP), dtype=jnp.float32) * s, 'wd': jax.random.normal(ks[4], (N_EXP, F_EXP, HID), dtype=jnp.float32) * s, 'sg': jax.random.normal(ks[5], (HID, F_SH), dtype=jnp.float32) * s, 'su': jax.random.normal(ks[6], (HID, F_SH), dtype=jnp.float32) * s, 'sd': jax.random.normal(ks[7], (F_SH, HID), dtype=jnp.float32) * s}
    _L0_ffn_all = _L0_ffn_setup()
    _L0_ffn_in = {k: v for k, v in _L0_ffn_all.items() if k in ('gate_w', 'wg', 'wu', 'wd', 'sg', 'su', 'sd')}
    del _L0_ffn_all
    return {'x': x, 'ctx_2048': ctx_2048, 'mask_BxS2_bf1': mask_BxS2_bf1, 'L0_xattn_Wq': _L0_xattn_in['Wq'], 'L0_xattn_Wk': _L0_xattn_in['Wk'], 'L0_xattn_Wv': _L0_xattn_in['Wv'], 'L0_xattn_Wo': _L0_xattn_in['Wo'], 'L0_ffn_gate_w': _L0_ffn_in['gate_w'], 'L0_ffn_wg': _L0_ffn_in['wg'], 'L0_ffn_wu': _L0_ffn_in['wu'], 'L0_ffn_wd': _L0_ffn_in['wd'], 'L0_ffn_sg': _L0_ffn_in['sg'], 'L0_ffn_su': _L0_ffn_in['su'], 'L0_ffn_sd': _L0_ffn_in['sd']}

def reference(x, ctx_2048, mask_BxS2_bf1, L0_xattn_Wq, L0_xattn_Wk, L0_xattn_Wv, L0_xattn_Wo, L0_ffn_gate_w, L0_ffn_wg, L0_ffn_wu, L0_ffn_wd, L0_ffn_sg, L0_ffn_su, L0_ffn_sd):
    import jax
    import jax.numpy as jnp

    def _L0_xattn_ref(query, key, value, mask, Wq, Wk, Wv, Wo):
        import jax, jax.numpy as jnp
        import numpy as np
        import math
        D_MODEL = 256
        N_Q_HEADS = 16
        N_KV_HEADS = 4
        HEAD_DIM = D_MODEL // N_Q_HEADS
        B = 4
        S = 128

        def _alibi_slopes(num_heads):
            n = 2 ** int(math.floor(math.log2(num_heads)))
            m0 = 2.0 ** (-8.0 / n)
            return m0 ** jnp.arange(1, n + 1, dtype=jnp.float32)
        b, q_len, d = query.shape
        kv_len = key.shape[1]
        G = N_KV_HEADS
        Hpg = N_Q_HEADS // G
        dh = HEAD_DIM
        Q = (query @ Wq).reshape(b, q_len, G, Hpg, dh)
        K = (key @ Wk).reshape(b, kv_len, G, dh)
        V = (value @ Wv).reshape(b, kv_len, G, dh)
        Q = Q / math.sqrt(dh)
        scores = jnp.einsum('bqghd,bkgd->bghqk', Q, K)
        rel = jnp.arange(kv_len, dtype=jnp.float32)[None, :] - jnp.arange(q_len, dtype=jnp.float32)[:, None]
        m = _alibi_slopes(N_Q_HEADS).reshape(1, G, Hpg, 1, 1)
        scores = scores + m * rel[None, None, None]
        neg = jnp.finfo(scores.dtype).min
        scores = jnp.where(mask[:, None, None, None, :], scores, neg)
        w = jax.nn.softmax(scores, axis=-1)
        out = jnp.einsum('bghqk,bkgd->bqghd', w, V)
        out = out.reshape(b, q_len, G * Hpg * dh)
        return out @ Wo

    def _L0_ffn_ref(hidden_states, gate_w, wg, wu, wd, sg, su, sd):
        import jax, jax.numpy as jnp
        import numpy as np
        HID = 256
        N_EXP = 32
        F_EXP = 96
        TOP_K = 6
        F_SH = 192
        B, S = (1, 128)
        orig_shape = hidden_states.shape
        x = hidden_states.reshape(-1, HID)
        scores = jax.nn.sigmoid(x @ gate_w)
        topk_w, topk_i = jax.lax.top_k(scores, TOP_K)
        topk_w = topk_w / (jnp.sum(topk_w, axis=-1, keepdims=True) + 1e-20)
        combine = jnp.sum(jax.nn.one_hot(topk_i, N_EXP, dtype=topk_w.dtype) * topk_w[..., None], axis=1)
        g = jnp.einsum('td,edf->tef', x, wg)
        u = jnp.einsum('td,edf->tef', x, wu)
        act = jax.nn.silu(g) * u
        routed = jnp.einsum('tef,efd,te->td', act, wd, combine)
        routed = routed.reshape(orig_shape)
        shared = jax.nn.silu(hidden_states @ sg) * (hidden_states @ su) @ sd
        return routed + shared
    x = x + _L0_xattn_ref(_layernorm(x, axis=-1), ctx_2048, ctx_2048, mask_BxS2_bf1, L0_xattn_Wq, L0_xattn_Wk, L0_xattn_Wv, L0_xattn_Wo)
    x = x + _L0_ffn_ref(_layernorm(x, axis=-1), L0_ffn_gate_w, L0_ffn_wg, L0_ffn_wu, L0_ffn_wd, L0_ffn_sg, L0_ffn_su, L0_ffn_sd)
    return x

_drawn_inputs = setup_inputs


def setup_inputs(seed=0):
    import zlib

    import numpy as np

    out = dict(_drawn_inputs(seed))
    spreads = {}
    factors = {'L0_ffn_gate_w': 8.0,
     'L0_ffn_wg': 8.0,
     'L0_ffn_wu': 8.0,
     'L0_ffn_wd': 8.0,
     'L0_ffn_sg': 5.01,
     'L0_ffn_su': 4.954,
     'L0_ffn_sd': 4.937}
    for name, (base, spread) in spreads.items():
        noise = np.random.default_rng([zlib.crc32(name.encode()), seed]).standard_normal(out[name].shape)
        drawn = base * np.exp(spread * noise) if base else spread * noise
        out[name] = jnp.asarray(drawn.astype(out[name].dtype))
    for name, factor in factors.items():
        out[name] = (out[name] * factor).astype(out[name].dtype)
    return out
```

```python
from contextlib import ExitStack

import numpy as np

import concourse.bass as bass
from concourse import mybir

F32 = mybir.dt.float32
BF16 = mybir.dt.bfloat16
U8 = mybir.dt.uint8
ALU = mybir.AluOpType
ACT = mybir.ActivationFunctionType
AX_X = mybir.AxisListType.X

B, NQ, D = 32, 56, 256
NK = 1500
G, J, DH = 4, 4, 16
H = G * J
T = B * NQ
NT = T // 128
BLK = 448
NBLK = T // BLK
E, TOPK, FE, FS = 32, 6, 96, 192
HID = E * FE + FS
NH = -(-HID // 128)
HP = NH * 128
EPS = 1e-5

THIRD = [(0, 512), (512, 512), (1024, NK - 1024)]
CHUNK = [(c, min(128, NK - c)) for c in range(0, NK, 128)]
NC = len(CHUNK)
QH = H * NQ
TQ = 2 * NQ
NU = 3 * 2 * G
UNITS = [3, 2, 2, 2, 2, 2, 2, 3, 3, 3, 0, 0]

NBAND = 6
BANDS = NBAND * DH
EXTRA = BANDS
MASKROW = EXTRA + 12
ROWS = MASKROW + 1
MASKED = -2.0 ** 100

VSTEPS = [1, 2, 4]
CREDIT = 2


def _dram_in(nc, name, shape, dt):
    return nc.dram_tensor(name, shape, dt, kind="ExternalInput").ap()


def build(nc, x_nat, x_tr, ctx_tr, mask, w_q, w_kv, w_o, gate_w, w_g, w_u, w_d, c_ident, c_identb, c_krows,
          c_qrows, c_sel, out_tr):
    ctx = ExitStack()
    with ctx:
        def sb(name, shape, dt, scope=ctx):
            return scope.enter_context(nc.sbuf_tensor(name, shape, dt))

        def sem(name):
            return ctx.enter_context(nc.semaphore(name))

        ident = sb("ident", [128, 128], F32)
        identb = sb("identb", [128, 128], BF16)
        wq = sb("wq", [128, 2, D], F32)
        wkv = sb("wkv", [128, 2, 128], F32)
        wo = sb("wo", [128, J, D], F32)
        gate = sb("gate", [128, 2, E], F32)
        resid = sb("resid", [128, 2, T], F32)
        attn = sb("attn", [128, J, T], F32)
        stats = sb("stats", [128, NT, 6], F32)
        mv = sb("mv", [128, NT, 2], F32)
        var = sb("var", [128, NT], F32)
        std = sb("std", [128, NT], F32)
        rstd = sb("rstd", [128, NT], F32)
        newt = sb("newt", [128, NT], F32)
        warm = sb("warm", [1, 2], F32)

        att = ExitStack()
        qst = sb("qst", [ROWS, H, T], BF16, att)
        kst = [sb(f"kst{p}", [ROWS, G, NK], BF16, att) for p in range(2)]
        kvin = [sb(f"kvin{p}", [128, 2, NK], F32, att) for p in range(2)]
        kvf = [sb(f"kvf{p}", [128, 512], F32, att) for p in range(2)]
        kparts = [sb(f"kparts{p}", [64, 3, 512], BF16, att) for p in range(2)]
        kres = sb("kres", [64, 512], F32, att)
        vaug = [sb(f"vaug{p}", [128, NC, G, 32], F32, att) for p in range(2)]
        probs = [sb(f"probs{p}", [128, QH], F32, att) for p in range(2)]
        qs = [sb(f"qs{p}", [ROWS, QH], BF16, att) for p in range(2)]
        qb = [sb(f"qb{p}", [ROWS, QH], BF16, att) for p in range(2)]
        zero = sb("zero", [ROWS, 1], BF16, att)
        maxp = sb("maxp", [TQ, 2 * G, 3], F32, att)
        nmax = sb("nmax", [TQ, 2 * G], F32, att)
        nres = sb("nres", [TQ, 2 * G], F32, att)
        nparts = sb("nparts", [TQ, 2 * G, 3], BF16, att)
        maskin = probs[0][:, :].bitcast(U8)[0:B, 0:NK]
        maskb = probs[1][:, :].bitcast(BF16)[0:B, 0:NK]
        qparts = sb("qparts", [128, 3, T], BF16, att)
        qf = [sb(f"qf{p}", [128, BLK], F32, att) for p in range(2)]
        qres = sb("qres", [128, BLK], F32, att)
        attn_flat = attn[:, :, :].rearrange("p j t -> p (j t)")
        xnat = attn_flat[:, 0:NT * D].rearrange("p (n d) -> p n d", d=D)
        xnT = attn_flat[:, NT * D:NT * D + 2 * T].rearrange("p (h t) -> p h t", h=2)
        att.close()

        wg = sb("wg", [128, 2, HP], F32)
        wu = sb("wu", [128, 2, HP], F32)
        wd = sb("wd", [128, NH, D], F32)
        x1nat, x2T = xnat, xnT
        ssum = sb("ssum", [128, J, BLK], F32)
        slog = sb("slog", [128, J, BLK], F32)
        srec = sb("srec", [128, J, BLK], F32)
        score = sb("score", [128, NT, E + 2], F32)
        top8 = sb("top8", [128, NT, 8], F32)
        rest = sb("rest", [128, NT, E + 2], F32)
        chosen = sb("chosen", [128, NT, E], F32)
        wsum = sb("wsum", [128, NT], F32)
        wrec = sb("wrec", [128, NT], F32)
        cres = sb("cres", [128, NT, E], F32)
        cparts = sb("cparts", [128, NT, 3 * E], BF16)
        combine = sb("combine", [3 * E + 1, T], BF16)
        sel = sb("sel", [3 * E + 1, HP], BF16)
        silu = [sb(f"silu{p}", [128, BLK], F32) for p in range(2)]
        gated = [sb(f"gated{p}", [128, BLK], F32) for p in range(2)]
        hidden = [sb(f"hidden{p}", [128, BLK], F32) for p in range(2)]

        stp = [ctx.enter_context(nc.psum_tensor(f"stp{p}", [128, 2, 512], F32)) for p in range(2)]
        sbk = [ctx.enter_context(nc.psum_tensor(f"sbk{p}", [128, 512], F32)) for p in range(2)]
        obk = ctx.enter_context(nc.psum_tensor("obk", [128, 512], F32))
        misc = ctx.enter_context(nc.psum_tensor("misc", [128, 512], F32))
        miscb = misc[:, :].bitcast(BF16)
        qbank = [stp[0][:, 0, :], stp[0][:, 1, :], stp[1][:, 0, :], stp[1][:, 1, :]]

        k_parts = nc.dram_tensor("k_parts", (2, NBAND, DH * G, NK), BF16, kind="Internal").ap()
        q_parts = nc.dram_tensor("q_parts", (2, NBAND, 128, T), BF16, kind="Internal").ap()
        mask_bias = nc.dram_tensor("mask_bias", (B, NK), BF16, kind="Internal").ap()

        x_in = sem("x_in")
        small_in = sem("small_in")
        mask_in = sem("mask_in")
        rows_in = sem("rows_in")
        mask_cut = sem("mask_cut")
        mask_out = sem("mask_out")
        ones_set = sem("ones_set")
        vec = sem("vec")
        var_done = sem("var_done")
        std_done = sem("std_done")
        xn_done = sem("xn_done")
        xt_ready = sem("xt_ready")
        xt_done = sem("xt_done")
        q_ready = sem("q_ready")
        q_out = sem("q_out")
        q_cut = sem("q_cut")
        qw_done = sem("qw_done")
        qst_in = sem("qst_in")
        kvin_in = [sem("kvin_in0"), sem("kvin_in1")]
        kv_ready = sem("kv_ready")
        kv_out = sem("kv_out")
        k_cut = sem("k_cut")
        kw_done = sem("kw_done")
        kst_in = [sem(f"kst_in{t}") for t in range(3)]
        vt_ready = sem("vt_ready")
        v_done = sem("v_done")
        s_ready = sem("s_ready")
        max_done = sem("max_done")
        nmax_step = sem("nmax_step")
        nmaxT_ready = sem("nmaxT_ready")
        qs_done = sem("qs_done")
        qb_done = sem("qb_done")
        qmax_done = sem("qmax_done")
        st_ready = sem("st_ready")
        exp_done = sem("exp_done")
        pv_ready = sem("pv_ready")
        o_done = sem("o_done")
        log_done = sem("log_done")
        sum_done = sem("sum_done")
        norm_done = sem("norm_done")
        y_ready = sem("y_ready")
        res_done = sem("res_done")
        x1t_ready = sem("x1t_ready")
        x1_done = sem("x1_done")
        lg_ready = sem("lg_ready")
        score_done = sem("score_done")
        cp_done = sem("cp_done")
        ct_ready = sem("ct_ready")
        ct_done = sem("ct_done")
        sel_in = sem("sel_in")
        NWP = 4
        WP = [(n * NH // NWP, (n + 1) * NH // NWP) for n in range(NWP)]
        w_in = [sem(f"w_in{n}") for n in range(NWP)]
        gu_ready = sem("gu_ready")
        silu_done = sem("silu_done")
        gated_done = sem("gated_done")
        hid_done = sem("hid_done")
        acc_ready = sem("acc_ready")
        out_done = sem("out_done")
        out_sent = sem("out_sent")

        block = ctx.enter_context(nc.Block())

        def over_batches(eng, part):
            part(-2, -1, 0, now=False, nxt=False, kv2=False, kv01=True)
            part(-1, -1, 1, now=False, nxt=True, kv2=True, kv01=True)
            with eng.Fori(0, B // 2 - 1) as i:
                for p in range(2):
                    part(2 * i + p, i, p, now=True, nxt=True, kv2=True, kv01=True)
            part(B - 2, B // 2 - 1, 0, now=True, nxt=True, kv2=True, kv01=False)
            part(B - 1, B // 2 - 1, 1, now=True, nxt=False, kv2=False, kv01=False)

        def thirds(kv2, kv01):
            return [(1, 2, 0)] * kv2 + [(2, 0, 4), (2, 1, 8)] * kv01

        UNIT_AT = [sum(UNITS[:c]) for c in range(NC)]

        @block.sync
        def _(sync):
            sync.dma_start(xnat, x_nat.rearrange("(n p) d -> p n d", p=128)).then_inc(x_in, 16)
            for dst, src in [(ident[:, :], c_ident), (identb[:, :], c_identb),
                             (wq[:, :, :], w_q.rearrange("(h p) n -> p h n", p=128)),
                             (wkv[:, :, :], w_kv.rearrange("(h p) n -> p h n", p=128)),
                             (wo[:, :, :], w_o), (gate[:, :, :], gate_w.rearrange("(h p) n -> p h n", p=128)),
                             (resid[:, :, :], x_tr.rearrange("(h p) t -> p h t", p=128))]:
                sync.dma_start(dst, src).then_inc(small_in, 16)
            for p in range(2):
                sync.dma_start(kvin[p][:, :, :], ctx_tr[p].rearrange("(h p) k -> p h k", p=128)) \
                    .then_inc(kvin_in[p], 16)
            sync.dma_start(maskin, mask).then_inc(mask_in, 16)
            for p in range(2):
                sync.dma_start(kst[p][EXTRA:MASKROW, :, :], c_krows).then_inc(rows_in, 16)
            sync.dma_start(qst[EXTRA:ROWS, :, :], c_qrows).then_inc(rows_in, 16)
            sync.wait_ge(mask_cut, 1)
            sync.dma_start(mask_bias, maskb).then_inc(mask_out, 16)
            sync.wait_ge(mask_out, 16)
            for m in range(2):
                sync.wait_ge(q_cut, 4 * NBLK * (m + 1))
                for band, part, n in [(0, 0, 3), (3, 1, 2), (5, 2, 1)]:
                    sync.dma_start(q_parts[m, band:band + n].rearrange("b r t -> r b t"),
                                   qparts[:, part:part + 1, :].to_broadcast([128, n, T])).then_inc(qw_done, 16)
                sync.wait_ge(qw_done, 48 * (m + 1))
                sync.dma_start(qst[0:BANDS, m * 8:m * 8 + 8, :],
                               q_parts[m].rearrange("b (d h) t -> (b d) h t", h=8)).then_inc(qst_in, 16)

            def part(b, i, p, now, nxt, kv2, kv01):
                if kv2 and kv01:
                    sync.wait_ge(kv_ready, 3 * (b + 2))
                    n = (p + 3) % 2
                    load_ctx(b + 3, n)
                for d, t, _ in thirds(kv2, kv01):
                    k0, ks = THIRD[t]
                    n = (p + d) % 2
                    k = 3 * (b + d) + t
                    if now:
                        sync.wait_ge(st_ready, 12 * b + (1 if d == 1 else 4 * t + 4))
                    sync.dma_start(kst[n][MASKROW:ROWS, :, k0:k0 + ks],
                                   row(mask_bias, b + d)[:, k0:k0 + ks].unsqueeze(1).to_broadcast([1, G, ks])) \
                        .then_inc(kst_in[t], 16)
                    sync.wait_ge(k_cut, 3 * k + 3)
                    for band, m in [(0, 3), (3, 2), (5, 1)]:
                        sync.dma_start(k_parts[n, band:band + m, :, k0:k0 + ks].rearrange("b r k -> r b k"),
                                       kparts[(n + t) % 2][:, 0:m, 0:ks]).then_inc(kw_done, 16)
                    sync.wait_ge(kw_done, 48 * (k + 1))
                    sync.dma_start(kst[n][0:BANDS, :, k0:k0 + ks],
                                   k_parts[n, :, :, k0:k0 + ks].rearrange("b (d g) k -> (b d) g k", g=G)) \
                        .then_inc(kst_in[t], 16)

            def row(a, r):
                return a[bass.ds(r, 1), :]

            def load_ctx(r, n):
                src = ctx_tr[bass.ds(r, 1)].rearrange("o (h p) k -> p (o h) k", p=128)
                sync.dma_start(kvin[n][:, :, :], src).then_inc(kvin_in[n], 16)

            over_batches(sync, part)

            sync.wait_ge(o_done, B + 1)
            sync.wait_ge(kvin_in[0], 16 * (B // 2 + 1))
            sync.wait_ge(kvin_in[1], 16 * (B // 2))
            sync.dma_start(sel[:, :], c_sel).then_inc(sel_in, 16)
            for n, (a, z) in enumerate(WP):
                for dst, src in [(wg, w_g), (wu, w_u)]:
                    sync.dma_start(dst[:, :, a * 128:z * 128],
                                   src[:, a * 128:z * 128].rearrange("(h p) n -> p h n", p=128)).then_inc(w_in[n], 16)
                sync.dma_start(wd[:, a:z, :], w_d[a * 128:z * 128, :].rearrange("(n p) d -> p n d", p=128)) \
                    .then_inc(w_in[n], 16)
            with sync.Fori(0, NBLK) as t:
                sync.wait_ge(out_done, t + 2)
                sync.dma_start(out_tr.rearrange("(h p) t -> p h t", p=128)[:, :, bass.ds(t * BLK, BLK)],
                               resid[:, :, bass.ds(t * BLK, BLK)]).then_inc(out_sent, 16)
            sync.wait_ge(out_sent, 16 * NBLK)

        @block.tensor
        def _(pe):
            def turn(src, n, banks, ready, before, base):
                pe.wait_ge(before, base + 2 * n + 2)
                if n >= 2:
                    pe.wait_ge(xt_done, base // 2 + n - 1)
                for a in range(2):
                    for h in range(2):
                        mm = pe.transpose(banks[n % 2][:, h * 256 + a * 128:h * 256 + a * 128 + 128],
                                          src[:, 2 * n + a, h * 128:h * 128 + 128], ident[:, :])
                mm.then_inc(ready, 1)

            pe.wait_ge(small_in, 16 * 7)
            for n in range(NT // 2):
                turn(xnat, n, sbk, xt_ready, xn_done, 0)
            pe.wait_ge(xt_done, NT // 2)
            for m in range(2):
                for t in range(NBLK):
                    if m:
                        pe.wait_ge(q_out, NBLK * (m - 1) + t + 1)
                    for h in range(2):
                        mm = pe.matmul(qbank[t][:, 0:BLK], wq[:, h, m * 128:m * 128 + 128],
                                       xnT[:, h, bass.ds(t * BLK, BLK)], start=(h == 0), stop=(h == 1))
                    mm.then_inc(q_ready, 1)

            def scores(b, p, c):
                k0, ks = CHUNK[c]
                if c == 0:
                    pe.wait_ge(qmax_done, b + 1)
                pe.wait_ge(exp_done, NC * b + c - 1 + CREDIT)
                for g in range(G):
                    mm = pe.matmul(stp[c % 2][0:ks, g // 2, (g % 2) * 224:(g % 2) * 224 + 224],
                                   kst[p][:, g, k0:k0 + ks], qb[p][:, g * 224:g * 224 + 224], start=True, stop=True)
                mm.then_inc(st_ready, 1)

            def values(b, p, c):
                ks = CHUNK[c][1]
                if c == 0:
                    pe.wait_ge(o_done, b + 1)
                if c % 4 == 0:
                    pe.wait_ge(v_done, 4 * b + VSTEPS[c // 4])
                pe.wait_ge(exp_done, NC * b + c + 1 + CREDIT)
                for g in range(G):
                    mm = pe.matmul(obk[32 * g:32 * g + 32, 0:224], vaug[p][0:ks, c, g, :],
                                   probs[c % 2][0:ks, g * 224:g * 224 + 224], start=(c == 0), stop=(c == NC - 1))
                if c == NC - 1:
                    mm.then_inc(pv_ready, 1)

            def unit(b, n, u):
                t, q = divmod(u, 2 * G)
                k0, ks = THIRD[t]
                if q == 0:
                    pe.wait_ge(kst_in[t], 32 * (b + 1))
                if u == 0:
                    pe.wait_ge(qs_done, b + 1)
                if u >= 2 or not isinstance(b, int) or b > 0:
                    pe.wait_ge(max_done, NU * b + u - 1)
                pe.matmul(sbk[u % 2][0:TQ, 0:ks], qs[n][:, q * TQ:q * TQ + TQ],
                          kst[n][:, q // 2, k0:k0 + ks], start=True, stop=True).then_inc(s_ready, 1)

            def part(b, i, p, now, nxt, kv2, kv01):
                at = {c: (d, t) for d, t, c in thirds(kv2, kv01)}
                for c in range(NC):
                    if now:
                        scores(b, p, c)
                    if nxt:
                        for u in range(UNIT_AT[c], UNIT_AT[c] + UNITS[c]):
                            unit(b + 1, (p + 1) % 2, u)
                    if c in at:
                        d, t = at[c]
                        n, k = (p + d) % 2, 3 * (b + d) + t
                        ts = THIRD[t][1]
                        k0 = THIRD[t][0]
                        if not (isinstance(k, int) and k == 0):
                            pe.wait_ge(v_done, 4 * (b + d) + (VSTEPS[t - 1] if t else 0))
                        if t != 1:
                            pe.wait_ge(kvin_in[n], 16 * (i + (p + d) // 2 + 1))
                        for h in range(2):
                            mm = pe.matmul(misc[:, 0:ts], wkv[:, h, :], kvin[n][:, h, k0:k0 + ts],
                                           start=(h == 0), stop=(h == 1))
                        mm.then_inc(kv_ready, 1)
                    if c >= 2 and c - 2 in at:
                        d, t = at[c - 2]
                        n, k = (p + d) % 2, 3 * (b + d) + t
                        pe.wait_ge(kv_out, 2 * k + 2)
                        for a in range(4):
                            k0, ks = CHUNK[4 * t + a]
                            mm = pe.transpose(misc[0:ks, a * 128:a * 128 + 128],
                                              kvf[(n + t) % 2][:, a * 128:a * 128 + ks], ident[:, :])
                        mm.then_inc(vt_ready, 1)
                    if now and c:
                        values(b, p, c - 1)
                if nxt:
                    pe.wait_ge(nmax_step, 5 * (b + 2))
                    pe.wait_ge(v_done, 4 * (b + 2) + (VSTEPS[1] if kv01 else 0))
                    for q in range(2 * G):
                        mm = pe.transpose(miscb[EXTRA:EXTRA + 3, q * TQ:q * TQ + TQ], nparts[:, q, :],
                                          identb[0:TQ, 0:TQ])
                    mm.then_inc(nmaxT_ready, 1)
                if now:
                    values(b, p, NC - 1)

            pe.wait_ge(q_out, 2 * NBLK)
            pe.wait_ge(rows_in, 48)
            over_batches(pe, part)

            for t in range(NBLK):
                pe.wait_ge(norm_done, t + 1)
                if t >= 2:
                    pe.wait_ge(res_done, t - 1)
                for h in range(2):
                    for j in range(J):
                        mm = pe.matmul(stp[t % 2][:, h, 0:BLK], wo[:, j, h * 128:h * 128 + 128],
                                       attn[:, j, bass.ds(t * BLK, BLK)], start=(j == 0), stop=(j == J - 1))
                mm.then_inc(y_ready, 1)
            pe.wait_ge(res_done, NBLK)
            for n in range(NT // 2):
                if n >= 2:
                    pe.wait_ge(x1_done, n - 1)
                for a in range(2):
                    for h in range(2):
                        c0 = (2 * n + a) * 128
                        mm = pe.transpose(sbk[n % 2][:, a * 256 + h * 128:a * 256 + h * 128 + 128],
                                          resid[:, h, c0:c0 + 128], ident[:, :])
                mm.then_inc(x1t_ready, 1)
            pe.wait_ge(x1_done, NT // 2)
            for n in range(NT // 2):
                turn(x1nat, n, sbk, xt_ready, xn_done, NT)
            pe.wait_ge(xt_done, NT)
            for n in range(NT):
                for h in range(2):
                    mm = pe.matmul(misc[:, n * E:n * E + E], x2T[:, h, n * 128:n * 128 + 128], gate[:, h, :],
                                   start=(h == 0), stop=(h == 1))
            mm.then_inc(lg_ready, 1)
            pe.wait_ge(cp_done, 1)
            pe.wait_ge(score_done, 1)
            combT = [obk[:, :].bitcast(BF16), misc[:, :].bitcast(BF16)]
            for n in range(NT):
                mm = pe.transpose(combT[n // 8][0:3 * E, n % 8 * 128:n % 8 * 128 + 128], cparts[:, n, :], identb[:, :])
            mm.then_inc(ct_ready, 1)
            pe.wait_ge(ct_done, 2)
            pe.wait_ge(sel_in, 16)

            def down(t, k):
                if k == 0:
                    pe.wait_ge(out_done, t + 1)
                pe.wait_ge(hid_done, NH * t + k + 1 + CREDIT)
                for h in range(2):
                    mm = pe.matmul([obk, misc][h][:, 0:BLK], wd[:, k, h * 128:h * 128 + 128], hidden[k % 2][:, :],
                                   start=(k == 0), stop=(k == NH - 1))
                if k == NH - 1:
                    mm.then_inc(acc_ready, 1)

            with pe.Fori(0, NBLK) as t:
                for k in range(NH):
                    n = next(n for n, (a, z) in enumerate(WP) if a <= k < z)
                    if k == WP[n][0]:
                        pe.wait_ge(w_in[n], 48)
                    pe.wait_ge(hid_done, NH * t + k - 1 + CREDIT)
                    for o, w in [(0, wg), (1, wu)]:
                        for h in range(2):
                            pe.matmul(stp[k % 2][:, o, 0:BLK], w[:, h, k * 128:k * 128 + 128],
                                      x2T[:, h, bass.ds(t * BLK, BLK)], start=(h == 0), stop=(h == 1))
                    pe.matmul(sbk[k % 2][:, 0:BLK], sel[:, k * 128:k * 128 + 128], combine[:, bass.ds(t * BLK, BLK)],
                              start=True, stop=True).then_inc(gu_ready, 1)
                    if k:
                        down(t, k - 1)
                down(t, NH - 1)

        @block.scalar
        def _(act):
            act.wait_ge(ones_set, 1)
            for n in range(CREDIT):
                nc.scalar.activation(warm[:, n:n + 1], warm[:, n:n + 1], ACT.Exp).then_inc(exp_done, 1)
            act.wait_ge(var_done, 1)
            nc.scalar.activation(std[:, :], var[:, :], ACT.Sqrt).then_inc(std_done, 1)
            for n in range(NT // 2):
                act.wait_ge(xt_ready, n + 1)
                nc.scalar.copy(xnT[:, :, n * 256:n * 256 + 256],
                               sbk[n % 2][:, :].rearrange("p (h t) -> p h t", h=2)).then_inc(xt_done, 1)
            for k in range(2 * NBLK):
                act.wait_ge(q_ready, k + 1)
                if k >= 2:
                    act.wait_ge(q_cut, 4 * (k - 1))
                nc.scalar.mul(qf[k % 2][:, :], qbank[k % NBLK][:, 0:BLK], DH ** -0.5).then_inc(q_out, 1)

            def part(b, i, p, now, nxt, kv2, kv01):
                at = {c: (d, t) for d, t, c in thirds(kv2, kv01)}
                for c in range(NC):
                    if now:
                        ks = CHUNK[c][1]
                        act.wait_ge(st_ready, NC * b + c + 1)
                        nc.scalar.activation(probs[c % 2][0:ks, :].rearrange("k (a n) -> k a n", a=2),
                                             stp[c % 2][0:ks, :, 0:448], ACT.Exp).then_inc(exp_done, 1)
                    if c in at:
                        d, t = at[c]
                        k = 3 * (b + d) + t
                        n = (p + d + t) % 2
                        ts = THIRD[t][1]
                        act.wait_ge(kv_ready, k + 1)
                        if not isinstance(k, int) or k >= 2:
                            act.wait_ge(vt_ready, k - 1)
                            act.wait_ge(k_cut, 3 * (k - 1))
                            act.wait_ge(kw_done, 48 * (k - 1))
                        nc.scalar.copy(kvf[n][:, 0:ts], misc[:, 0:ts]).then_inc(kv_out, 1)
                        nc.scalar.copy(kparts[n][:, 0, 0:ts], misc[0:64, 0:ts]).then_inc(kv_out, 1)

            over_batches(act, part)

            for t in range(NBLK):
                act.wait_ge(sum_done, t + 1)
                if t:
                    act.wait_ge(norm_done, t)
                nc.scalar.activation(slog[:, :, :], ssum[:, :, :], ACT.Ln).then_inc(log_done, 1)
                act.wait_ge(log_done, 2 * t + 1)
                nc.scalar.activation(srec[:, :, :], slog[:, :, :], ACT.Exp, scale=-1.0).then_inc(log_done, 1)
            for n in range(NT // 2):
                act.wait_ge(x1t_ready, n + 1)
                nc.scalar.copy(x1nat[:, 2 * n:2 * n + 2, :],
                               sbk[n % 2][:, :].rearrange("p (a d) -> p a d", a=2)).then_inc(x1_done, 1)
            act.wait_ge(var_done, 2)
            nc.scalar.activation(std[:, :], var[:, :], ACT.Sqrt).then_inc(std_done, 1)
            for n in range(NT // 2):
                act.wait_ge(xt_ready, NT // 2 + n + 1)
                nc.scalar.copy(x2T[:, :, n * 256:n * 256 + 256],
                               sbk[n % 2][:, :].rearrange("p (h t) -> p h t", h=2)).then_inc(xt_done, 1)
            act.wait_ge(lg_ready, 1)
            nc.scalar.activation(score[:, :, 0:E], misc[:, 0:NT * E].rearrange("p (n e) -> p n e", e=E),
                                 ACT.Sigmoid).then_inc(score_done, 1)
            with act.Fori(0, NBLK) as t:
                for k in range(NH):
                    act.wait_ge(gu_ready, NH * t + k + 1)
                    nc.scalar.activation(silu[k % 2][:, :], stp[k % 2][:, 0, 0:BLK], ACT.Silu).then_inc(silu_done, 1)

        @block.gpsimd
        def _(pool):
            nc.gpsimd.memset(warm[:, :], 0.0).then_inc(ones_set, 1)
            nc.gpsimd.memset(zero[:, :], 0.0).then_inc(ones_set, 1)
            for n in range(2):
                nc.gpsimd.memset(vaug[n][:, :, :, DH:32], 1.0).then_inc(ones_set, 1)

            def part(b, i, p, now, nxt, kv2, kv01):
                def cut(d, t):
                    k = 3 * (b + d) + t
                    n = (p + d + t) % 2
                    ts = THIRD[t][1]
                    pool.wait_ge(kv_out, 2 * k + 2)
                    if not (isinstance(k, int) and k == 0):
                        pool.wait_ge(k_cut, 3 * k)
                    nc.gpsimd.tensor_tensor(kres[:, 0:ts], kvf[n][0:64, 0:ts], kparts[n][:, 0, 0:ts],
                                            ALU.subtract).then_inc(k_cut, 1)
                    nc.gpsimd.tensor_tensor(kparts[n][:, 1, 0:ts], kvf[n][0:64, 0:ts], kparts[n][:, 0, 0:ts],
                                            ALU.subtract) \
                        .then_inc(k_cut, 1)
                    pool.wait_ge(k_cut, 3 * k + 2)
                    nc.gpsimd.tensor_tensor(kparts[n][:, 2, 0:ts], kres[:, 0:ts], kparts[n][:, 1, 0:ts],
                                            ALU.subtract).then_inc(k_cut, 1)

                if kv2:
                    cut(1, 2)
                if kv01:
                    cut(2, 0)
                    cut(2, 1)
                    if now:
                        pool.wait_ge(st_ready, NC * b + 1)
                        pool.wait_ge(qb_done, b + 1)
                    pool.wait_ge(ones_set, 4)
                    pool.wait_ge(rows_in, 48)
                    pool.wait_ge(qst_in, 32)
                    q = qst[:, :, bass.ds((b + 2) * NQ, NQ)]
                    nc.gpsimd.tensor_tensor(qs[p][:, :].rearrange("r (h q) -> r h q", h=H), q,
                                            zero[:, :].unsqueeze(2).to_broadcast([ROWS, H, NQ]), ALU.add) \
                        .then_inc(qs_done, 1)

            over_batches(pool, part)

        @block.vector
        def _(dve):
            step = [0]

            def own(ins):
                ins.then_inc(vec, 1)
                step[0] += 1
                return step[0]

            dve.wait_ge(mask_in, 16)
            nc.vector.tensor_scalar(maskb, maskin, -1.0, -MASKED, ALU.add, ALU.mult) \
                .then_inc(mask_cut, 1)

            def layer_norm(x, turn):
                for n in range(NT):
                    last = own(nc.vector.bn_stats(stats[:, n, :], x[:, n, :]))
                dve.wait_ge(vec, last)
                for n in range(NT):
                    last = own(nc.vector.bn_aggr(mv[:, n, :], stats[:, n, :]))
                dve.wait_ge(vec, last)
                nc.vector.tensor_scalar(var[:, :], mv[:, :, 1], EPS, None, ALU.add).then_inc(var_done, 1)
                dve.wait_ge(std_done, turn)
                dve.wait_ge(vec, own(nc.vector.reciprocal(rstd[:, :], std[:, :])))
                dve.wait_ge(vec, own(nc.vector.tensor_tensor(newt[:, :], rstd[:, :], rstd[:, :], ALU.mult)))
                dve.wait_ge(vec, own(nc.vector.tensor_tensor(newt[:, :], newt[:, :], var[:, :], ALU.mult)))
                dve.wait_ge(vec, own(nc.vector.tensor_scalar(newt[:, :], newt[:, :], -0.5, 1.5, ALU.mult, ALU.add)))
                dve.wait_ge(vec, own(nc.vector.tensor_tensor(rstd[:, :], rstd[:, :], newt[:, :], ALU.mult)))
                for n in range(NT):
                    nc.vector.tensor_scalar(x[:, n, :], x[:, n, :], mv[:, n, 0:1], rstd[:, n:n + 1],
                                            ALU.subtract, ALU.mult).then_inc(xn_done, 1)

            dve.wait_ge(x_in, 16)
            layer_norm(xnat, 1)
            for k in range(2 * NBLK):
                m, t = divmod(k, NBLK)
                c = slice(t * BLK, t * BLK + BLK)
                dve.wait_ge(q_out, k + 1)
                if m and t == 0:
                    dve.wait_ge(qw_done, 48)
                nc.vector.tensor_copy(qparts[:, 0, c], qf[k % 2][:, :]).then_inc(q_cut, 1)
                dve.wait_ge(q_cut, 4 * k + 1)
                nc.vector.tensor_tensor(qres[:, :], qf[k % 2][:, :], qparts[:, 0, c], ALU.subtract).then_inc(q_cut, 1)
                dve.wait_ge(q_cut, 4 * k + 2)
                nc.vector.tensor_copy(qparts[:, 1, c], qres[:, :]).then_inc(q_cut, 1)
                dve.wait_ge(q_cut, 4 * k + 3)
                nc.vector.tensor_tensor(qparts[:, 2, c], qres[:, :], qparts[:, 1, c], ALU.subtract).then_inc(q_cut, 1)
                dve.wait_ge(q_cut, 4 * k + 4)
            nc.vector.memset(nmax[:, :], 0.0).then_inc(o_done, 1)
            dve.wait_ge(o_done, 1)
            dve.wait_ge(ones_set, 4)

            def part(b, i, p, now, nxt, kv2, kv01):
                at = {c: (d, t) for d, t, c in thirds(kv2, kv01)}
                bn = b + 1
                for c in range(NC):
                    if nxt:
                        for u in range(UNIT_AT[c], UNIT_AT[c] + UNITS[c]):
                            t, q = divmod(u, 2 * G)
                            dve.wait_ge(s_ready, NU * bn + u + 1)
                            nc.vector.tensor_reduce(maxp[:, q, t:t + 1], sbk[u % 2][0:TQ, 0:THIRD[t][1]], AX_X,
                                                    ALU.max).then_inc(max_done, 1)
                    if c >= 2 and c - 2 in at:
                        d, t = at[c - 2]
                        n = (p + d) % 2
                        dve.wait_ge(vt_ready, 3 * (b + d) + t + 1)
                        for a, z, ks in ([(0, 4, 128)] if t < 2 else [(0, 3, 128), (3, 4, CHUNK[-1][1])]):
                            nc.vector.tensor_copy(vaug[n][0:ks, 4 * t + a:4 * t + z, :, 0:DH],
                                                  misc[0:ks, :].rearrange("k (c w g d) -> k c w g d", w=2, g=G, d=DH)
                                                  [:, a:z, 1]) \
                                .then_inc(v_done, 1)
                    if nxt and c == NC - 3:
                        dve.wait_ge(max_done, NU * (bn + 1))
                        nc.vector.tensor_reduce(nmax[:, :], maxp[:, :, :], AX_X, ALU.max, negate=True) \
                            .then_inc(nmax_step, 1)
                        dve.wait_ge(nmax_step, 5 * bn + 1)
                        nc.vector.tensor_copy(nparts[:, :, 0], nmax[:, :]).then_inc(nmax_step, 1)
                        dve.wait_ge(nmax_step, 5 * bn + 2)
                        nc.vector.tensor_tensor(nres[:, :], nmax[:, :], nparts[:, :, 0], ALU.subtract) \
                            .then_inc(nmax_step, 1)
                        dve.wait_ge(nmax_step, 5 * bn + 3)
                        nc.vector.tensor_copy(nparts[:, :, 1], nres[:, :]).then_inc(nmax_step, 1)
                        dve.wait_ge(nmax_step, 5 * bn + 4)
                        nc.vector.tensor_tensor(nparts[:, :, 2], nres[:, :], nparts[:, :, 1], ALU.subtract) \
                            .then_inc(nmax_step, 1)
                if nxt:
                    dve.wait_ge(qs_done, bn + 1)
                    if now:
                        dve.wait_ge(st_ready, NC * b + 1)
                    nc.vector.tensor_copy(qb[(p + 1) % 2][:, :], qs[(p + 1) % 2][:, :]).then_inc(qb_done, 1)
                    dve.wait_ge(nmaxT_ready, bn + 1)
                    dve.wait_ge(qb_done, bn + 1)
                    nc.vector.tensor_copy(qb[(p + 1) % 2][EXTRA:EXTRA + 3, :], miscb[EXTRA:EXTRA + 3, 0:QH]) \
                        .then_inc(qmax_done, 1)
                if now:
                    dve.wait_ge(pv_ready, b + 1)
                    nc.vector.tensor_copy(attn[:, :, bass.ds(b * NQ, NQ)],
                                          obk[:, 0:224].rearrange("p (j q) -> p j q", j=J)).then_inc(o_done, 1)

            over_batches(dve, part)

            dve.wait_ge(o_done, B + 1)
            dve.wait_ge(kvin_in[0], 16 * (B // 2 + 1))
            dve.wait_ge(kvin_in[1], 16 * (B // 2))
            up = list(range(16, 32)) * 2

            def take_sum(t):
                if t:
                    dve.wait_ge(norm_done, t)
                nc.vector.stream_shuffle(ssum[:, :, :], attn[:, :, bass.ds(t * BLK, BLK)], up).then_inc(sum_done, 1)

            take_sum(0)
            for t in range(NBLK):
                o = attn[:, :, bass.ds(t * BLK, BLK)]
                dve.wait_ge(sum_done, t + 1)
                dve.wait_ge(log_done, 2 * t + 2)
                dve.wait_ge(vec, own(nc.vector.tensor_tensor(slog[:, :, :], ssum[:, :, :], srec[:, :, :], ALU.mult)))
                dve.wait_ge(vec, own(nc.vector.scalar_tensor_tensor(
                    out=srec[:, :, :], in0=slog[:, :, :], scalar=-2.0, in1=srec[:, :, :], op0=ALU.add, op1=ALU.mult)))
                nc.vector.scalar_tensor_tensor(out=o, in0=o, scalar=-1.0, in1=srec[:, :, :], op0=ALU.mult,
                                               op1=ALU.mult).then_inc(norm_done, 1)
                if t + 1 < NBLK:
                    take_sum(t + 1)
                dve.wait_ge(y_ready, t + 1)
                r = resid[:, :, bass.ds(t * BLK, BLK)]
                nc.vector.tensor_tensor(r, r, stp[t % 2][:, :, 0:BLK], ALU.add).then_inc(res_done, 1)
            dve.wait_ge(x1_done, NT // 2)
            layer_norm(x1nat, 2)

            own(nc.vector.memset(combine[3 * E:3 * E + 1, :], 1.0))
            dve.wait_ge(vec, own(nc.vector.memset(score[:, :, E:E + 2], 2.0)))
            dve.wait_ge(score_done, 1)
            for n in range(NT):
                last = own(nc.vector.max(top8[:, n, :], score[:, n, :]))
            dve.wait_ge(vec, last)
            for n in range(NT):
                last = own(nc.vector.match_replace(rest[:, n, :], top8[:, n, :], score[:, n, :], -1.0))
            own(nc.vector.tensor_reduce(wsum[:, :], top8[:, :, 2:8], AX_X, ALU.add))
            dve.wait_ge(vec, step[0])
            own(nc.vector.scalar_tensor_tensor(out=chosen[:, :, :], in0=rest[:, :, 0:E], scalar=0.0,
                                               in1=score[:, :, 0:E], op0=ALU.is_lt, op1=ALU.mult))
            dve.wait_ge(vec, own(nc.vector.tensor_scalar(wsum[:, :], wsum[:, :], 1e-20, None, ALU.add)))
            dve.wait_ge(vec, own(nc.vector.reciprocal(wrec[:, :], wsum[:, :])))
            dve.wait_ge(vec, own(nc.vector.tensor_tensor(chosen[:, :, :], chosen[:, :, :],
                                                         wrec[:, :].unsqueeze(2).to_broadcast([128, NT, E]), ALU.mult)))
            dve.wait_ge(vec, own(nc.vector.tensor_copy(cparts[:, :, 0:E], chosen[:, :, :])))
            dve.wait_ge(vec, own(nc.vector.tensor_tensor(cres[:, :, :], chosen[:, :, :], cparts[:, :, 0:E],
                                                         ALU.subtract)))
            dve.wait_ge(vec, own(nc.vector.tensor_copy(cparts[:, :, E:2 * E], cres[:, :, :])))
            nc.vector.tensor_tensor(cparts[:, :, 2 * E:3 * E], cres[:, :, :], cparts[:, :, E:2 * E], ALU.subtract) \
                .then_inc(cp_done, 1)
            dve.wait_ge(ct_ready, 1)
            for n, bank, w in [(0, obk, 1024), (1, misc, T - 1024)]:
                nc.vector.tensor_copy(combine[0:3 * E, n * 1024:n * 1024 + w],
                                      bank[:, :].bitcast(BF16)[0:3 * E, 0:w]).then_inc(ct_done, 1)
            dve.wait_ge(ct_done, 2)
            for n in range(CREDIT):
                nc.vector.memset(gated[n][:, 0:1], 0.0).then_inc(hid_done, 1)
            nc.vector.memset(hidden[0][:, 0:1], 0.0).then_inc(out_done, 1)
            dve.wait_ge(hid_done, CREDIT)
            dve.wait_ge(out_done, 1)

            with dve.Fori(0, NBLK) as t:
                for k in range(NH):
                    dve.wait_ge(silu_done, NH * t + k + 1)
                    nc.vector.tensor_tensor(gated[k % 2][:, :], silu[k % 2][:, :], stp[k % 2][:, 1, 0:BLK],
                                            ALU.mult).then_inc(gated_done, 1)
                    dve.wait_ge(gated_done, NH * t + k + 1)
                    nc.vector.tensor_tensor(hidden[k % 2][:, :], gated[k % 2][:, :], sbk[k % 2][:, 0:BLK],
                                            ALU.mult).then_inc(hid_done, 1)
                dve.wait_ge(acc_ready, t + 1)
                for h in range(2):
                    r = resid[:, h, bass.ds(t * BLK, BLK)]
                    ins = nc.vector.tensor_tensor(r, r, [obk, misc][h][:, 0:BLK], ALU.add)
                    if h == 0:
                        ins.then_inc(vec, 1)
                ins.then_inc(out_done, 1)


NP_BF16 = np.dtype(mybir.dt.np(BF16))


def _bf16_parts(a):
    a = np.asarray(a, np.float64)
    parts = []
    for _ in range(3):
        h = a.astype(NP_BF16)
        parts.append(h)
        a = a - h.astype(np.float64)
    return parts


def _constants():
    bf = NP_BF16
    slope = (np.float32(2.0 ** (-8.0 / H)) ** np.arange(1, H + 1, dtype=np.float32)).astype(np.float32)
    slope_parts = _bf16_parts(slope)
    q = np.arange(NQ, dtype=np.float64)
    shift_parts = _bf16_parts(-(slope.astype(np.float64)[:, None] * q[None, :]))
    qrows = np.zeros((ROWS - EXTRA, H, B, NQ), bf)
    for n in range(3):
        qrows[3 + n] = shift_parts[n][:, None, :]
        qrows[6 + n] = slope_parts[n][:, None, None]
        qrows[9 + n] = slope_parts[n][:, None, None]
    qrows[12] = 1.0
    keys = np.arange(NK)
    krows = np.zeros((12, G, NK), bf)
    krows[0:6] = 1.0
    krows[6:9] = (keys // 8 * 8).astype(np.float32)
    krows[9:12] = (keys % 8).astype(np.float32)
    sel = np.zeros((3 * E + 1, HP), bf)
    for e in range(E):
        for n in range(3):
            sel[n * E + e, e * FE:(e + 1) * FE] = 1.0
    sel[3 * E, E * FE:HID] = 1.0
    return {"c_ident": np.eye(128, dtype=np.float32), "c_identb": np.eye(128, dtype=np.float32).astype(bf),
            "c_krows": krows, "c_qrows": qrows.reshape(ROWS - EXTRA, H, T), "c_sel": sel}


def kernel(x, ctx_2048, mask_BxS2_bf1, L0_xattn_Wq, L0_xattn_Wk, L0_xattn_Wv, L0_xattn_Wo, L0_ffn_gate_w,
           L0_ffn_wg, L0_ffn_wu, L0_ffn_wd, L0_ffn_sg, L0_ffn_su, L0_ffn_sd):
    import concourse.bacc as bacc
    from concourse.bass_utils import run_bass_kernel_spmd

    def f(a):
        return np.asarray(a)

    def wide(routed, shared):
        a = np.concatenate([f(routed).transpose(1, 0, 2).reshape(D, E * FE), f(shared)], 1)
        return np.pad(a, ((0, 0), (0, HP - HID)))

    x2 = f(x).reshape(T, D)
    wq = f(L0_xattn_Wq).reshape(D, 2, 8, DH).transpose(0, 1, 3, 2).reshape(D, D)
    wk = f(L0_xattn_Wk).reshape(D, G, DH).transpose(0, 2, 1).reshape(D, G * DH)
    wo = np.pad(f(L0_xattn_Wo).reshape(G, J, DH, D).transpose(0, 2, 1, 3), ((0, 0), (0, DH), (0, 0), (0, 0)))
    arrays = {
        "x_nat": x2,
        "x_tr": x2.T,
        "ctx_tr": np.pad(f(ctx_2048).transpose(0, 2, 1), ((0, 1), (0, 0), (0, 0))),
        "mask": f(mask_BxS2_bf1).view(np.uint8),
        "w_q": wq,
        "w_kv": np.concatenate([wk, f(L0_xattn_Wv)], 1),
        "w_o": wo.reshape(128, J, D),
        "gate_w": f(L0_ffn_gate_w),
        "w_g": wide(L0_ffn_wg, L0_ffn_sg),
        "w_u": wide(L0_ffn_wu, L0_ffn_su),
        "w_d": np.pad(np.concatenate([f(L0_ffn_wd).reshape(E * FE, D), f(L0_ffn_sd)], 0), ((0, HP - HID), (0, 0))),
        **_constants(),
    }
    arrays = {n: np.ascontiguousarray(a) for n, a in arrays.items()}
    nc = bacc.Bacc("TRN2", target_bir_lowering=False, num_devices=1)
    aps = [_dram_in(nc, n, a.shape, mybir.dt.from_np(a.dtype)) for n, a in arrays.items()]
    out = nc.dram_tensor("out_tr", (D, T), F32, kind="ExternalOutput").ap()
    build(nc, *aps, out)
    r = run_bass_kernel_spmd(nc, [arrays], core_ids=[0])
    return np.ascontiguousarray(r.results[0]["out_tr"].T).reshape(B, NQ, D)
```

```python
from contextlib import ExitStack

import numpy as np

import concourse.bass as bass
from concourse import mybir

F32 = mybir.dt.float32
BF16 = mybir.dt.bfloat16
U8 = mybir.dt.uint8
F32R = mybir.dt.float32r
ALU = mybir.AluOpType
ACT = mybir.ActivationFunctionType
AX_X = mybir.AxisListType.X

B, NQ, D = 32, 56, 256
NK = 1500
G, J, DH = 4, 4, 16
H = G * J
T = B * NQ
NT = T // 128
BLK = 448
NBLK = T // BLK
E, TOPK, FE, FS = 32, 6, 96, 192
HID = E * FE + FS
NH = -(-HID // 128)
HP = NH * 128
EPS = 1e-5

THIRD = [(0, 512), (512, 512), (1024, NK - 1024)]
CHUNK = [(c, min(128, NK - c)) for c in range(0, NK, 128)]
NC = len(CHUNK)
QH = H * NQ
TQ = 2 * NQ
NU = 3 * 2 * G


def batch_order():
    cost = {"st": 36, "pv": 41, "kv": 86, "vt": 22, "last": 41, "mx": 15, "qb": 0, "o": 0}
    work = []
    for c in range(NC):
        if c == NC - 1:
            work.append(("mx",))
        work.append(("st", c))
        if c == 0:
            work += [("last",), ("o", 0), ("vt", 2)]
        if c in (2, 3, 4):
            work.append(("o", c - 1))
        if c == 5:
            work.append(("qb",))
        if c in KV_STEPS:
            work.append(("kv", KV_STEPS.index(c), 0))
        if c:
            work.append(("pv", c - 1))
        if c in KV_STEPS:
            work.append(("kv", KV_STEPS.index(c), 1))
        if c in (4, 8):
            work.append(("vt", c // 4 - 1))
    last = sum(cost[w[0]] for w in work) - UNITS_END
    order, done, n = [], 0, 0
    for w in work:
        order.append(w)
        done += cost[w[0]]
        burst = 0
        while n < NU and burst < UNITS_BURST and done >= UNITS_BEGIN + (last - UNITS_BEGIN) * n / (NU - 1):
            order.append(("u", n))
            n += 1
            burst += 1
    assert n == NU
    return order


UNITS_BEGIN, UNITS_END, UNITS_BURST = 80, 330, 2
KV_STEPS = (2, 6, 10)

ORDER = batch_order()

NBAND = 6
BANDS = NBAND * DH
EXTRA = BANDS
MASKROW = EXTRA + 12
ROWS = MASKROW + 1
MASKED = -2.0 ** 100

VSTEPS = [1, 2, 4]
UP = list(range(16, 32)) * 2
CREDIT = 2


def _dram_in(nc, name, shape, dt):
    return nc.dram_tensor(name, shape, dt, kind="ExternalInput").ap()


def build(nc, x_nat, x_tr, ctx_tr, mask, w_q, w_kv, w_o, gate_w, w_moe, c_ident, c_identb, c_krows,
          c_qrows, c_sel, out_tr):
    ctx = ExitStack()
    with ctx:
        def sb(name, shape, dt, scope=ctx):
            return scope.enter_context(nc.sbuf_tensor(name, shape, dt))

        def sem(name):
            return ctx.enter_context(nc.semaphore(name))

        ident = sb("ident", [128, 128], F32)
        identb = sb("identb", [128, 128], BF16)
        wq = sb("wq", [128, 2, D], F32)
        wkv = sb("wkv", [128, 2, 128], F32)
        wo = sb("wo", [128, J, D], F32)
        gate = sb("gate", [128, 2, E], F32)
        resid = sb("resid", [128, 2, T], F32)
        attn = sb("attn", [128, J, T], F32)
        stats = sb("stats", [128, NT, 6], F32)
        mv = sb("mv", [128, NT, 2], F32)
        var = sb("var", [128, NT], F32)
        std = sb("std", [128, NT], F32)
        rstd = sb("rstd", [128, NT], F32)
        newt = sb("newt", [128, NT], F32)
        warm = sb("warm", [1, 2], F32)

        att = ExitStack()
        qst = sb("qst", [ROWS, H, T], BF16, att)
        kvin = [sb(f"kvin{p}", [128, 2, NK], F32, att) for p in range(2)]
        kst = [sb(f"kst{p}", [ROWS, G, NK], BF16, att) for p in range(2)]
        kvf = [sb(f"kvf{p}", [128, 512], F32, att) for p in range(2)]
        kparts = [sb(f"kparts{p}", [64, 3, 512], BF16, att) for p in range(2)]
        kres = sb("kres", [64, 512], F32, att)
        vaug = [sb(f"vaug{p}", [128, NC, G, 32], F32, att) for p in range(2)]
        probs = [sb(f"probs{p}", [128, QH], F32, att) for p in range(2)]
        qs = [sb(f"qs{p}", [ROWS, QH], BF16, att) for p in range(2)]
        qb = [sb(f"qb{p}", [ROWS, QH], BF16, att) for p in range(2)]
        zero = sb("zero", [ROWS, 1], BF16, att)
        maxp = sb("maxp", [TQ, 2 * G, 3], F32, att)
        nmax = sb("nmax", [TQ, 2 * G], F32, att)
        nres = sb("nres", [TQ, 2 * G], F32, att)
        nparts = sb("nparts", [TQ, 2 * G, 3], BF16, att)
        maskin = probs[0][:, :].bitcast(U8)[0:B, 0:NK]
        maskb = probs[1][:, :].bitcast(BF16)[0:B, 0:NK]
        qparts = sb("qparts", [128, 3, T], BF16, att)
        qf = [sb(f"qf{p}", [128, BLK], F32, att) for p in range(2)]
        qres = sb("qres", [128, BLK], F32, att)
        ssum, srec = (qf[p][:, 0:224] for p in range(2))
        attn_flat = attn[:, :, :].rearrange("p j t -> p (j t)")
        xnat = attn_flat[:, 0:NT * D].rearrange("p (n d) -> p n d", d=D)
        xnT = attn_flat[:, NT * D:NT * D + 2 * T].rearrange("p (h t) -> p h t", h=2)
        att.close()

        wmoe = sb("wmoe", [128, NH, 6, 128], F32)
        assert NH * 6 * 128 * 4 <= H * T * 2 + 2 * 2 * NK * 4
        x1nat, x2T = xnat, xnT
        score = sb("score", [128, NT, E + 2], F32)
        top8 = sb("top8", [128, NT, 8], F32)
        rest = sb("rest", [128, NT, E + 2], F32)
        chosen = sb("chosen", [128, NT, E], F32)
        wsum = sb("wsum", [128, NT], F32)
        wrec = sb("wrec", [128, NT], F32)
        cres = sb("cres", [128, NT, E], F32)
        cparts = sb("cparts", [128, NT, 3 * E], BF16)
        combine = sb("combine", [3 * E + 1, T], BF16)
        sel = sb("sel", [3 * E + 1, HP], BF16)
        silu = [sb(f"silu{p}", [128, BLK], F32) for p in range(2)]
        gated = sb("gated", [128, BLK], F32)
        hid = sb("hid", [128, BLK], F32)
        x2p = [sb(f"x2p{a}", [128, 2, T], F32R) for a in range(2)]
        hidp = [[sb(f"hidp{p}{a}", [128, BLK], F32R) for a in range(2)] for p in range(2)]
        wgup = [[sb(f"wgup{p}{a}", [128, 4, 128], F32R) for a in range(2)] for p in range(2)]
        wdp = [[sb(f"wdp{p}{a}", [128, 2, 128], F32R) for a in range(2)] for p in range(2)]

        stp = [ctx.enter_context(nc.psum_tensor(f"stp{p}", [128, 2, 512], F32)) for p in range(2)]
        sbk = [ctx.enter_context(nc.psum_tensor(f"sbk{p}", [128, 512], F32)) for p in range(2)]
        obk = ctx.enter_context(nc.psum_tensor("obk", [128, 512], F32))
        misc = ctx.enter_context(nc.psum_tensor("misc", [128, 512], F32))
        sbkb = sbk[0][:, :].bitcast(BF16)
        qbank = [stp[0][:, 0, :], stp[0][:, 1, :], stp[1][:, 0, :], stp[1][:, 1, :]]

        k_parts = nc.dram_tensor("k_parts", (2, NBAND, DH * G, NK), BF16, kind="Internal").ap()
        q_parts = nc.dram_tensor("q_parts", (2, NBAND, 128, T), BF16, kind="Internal").ap()
        mask_bias = nc.dram_tensor("mask_bias", (B, NK), BF16, kind="Internal").ap()

        x_in = sem("x_in")
        small_in = sem("small_in")
        mask_in = sem("mask_in")
        rows_in = sem("rows_in")
        mask_cut = sem("mask_cut")
        mask_out = sem("mask_out")
        ones_set = sem("ones_set")
        vec = sem("vec")
        var_done = sem("var_done")
        std_done = sem("std_done")
        xn_done = sem("xn_done")
        xt_ready = sem("xt_ready")
        xt_done = sem("xt_done")
        q_ready = sem("q_ready")
        q_out = sem("q_out")
        q_cut = sem("q_cut")
        qw_done = sem("qw_done")
        qst_in = sem("qst_in")
        kvin_in = [sem("kvin_in0"), sem("kvin_in1")]
        kv_ready = sem("kv_ready")
        kv_out = sem("kv_out")
        k_cut = sem("k_cut")
        kw_done = sem("kw_done")
        kst_in = [sem(f"kst_in{t}") for t in range(3)]
        vt_ready = sem("vt_ready")
        v_done = sem("v_done")
        s_ready = sem("s_ready")
        max_done = sem("max_done")
        nmax_step = sem("nmax_step")
        nmaxT_ready = sem("nmaxT_ready")
        qs_done = sem("qs_done")
        qb_done = sem("qb_done")
        qmax_done = sem("qmax_done")
        st_ready = sem("st_ready")
        exp_done = sem("exp_done")
        pv_ready = sem("pv_ready")
        o_done = sem("o_done")
        norm_step = sem("norm_step")
        y_ready = sem("y_ready")
        res_done = sem("res_done")
        x1t_ready = sem("x1t_ready")
        x1_done = sem("x1_done")
        lg_ready = sem("lg_ready")
        score_done = sem("score_done")
        cp_done = sem("cp_done")
        ct_ready = sem("ct_ready")
        ct_done = sem("ct_done")
        sel_in = sem("sel_in")
        NWP = 4
        WP = [(n * NH // NWP, (n + 1) * NH // NWP) for n in range(NWP)]
        w_in = [sem(f"w_in{n}") for n in range(NWP)]
        gu_ready = sem("gu_ready")
        x2_high = sem("x2_high")
        x2_cut = sem("x2_cut")
        gu_cut = [sem("gu_high"), sem("gu_low")]
        d_cut = [sem("d_high"), sem("d_low")]
        silu_done = sem("silu_done")
        hid_step = sem("hid_step")
        down_done = sem("down_done")
        out_done = sem("out_done")
        out_sent = sem("out_sent")

        block = ctx.enter_context(nc.Block())

        def over_batches(eng, part):
            part(-2, -1, 0, now=False, nxt=False, kv=True, end=False)
            part(-1, -1, 1, now=False, nxt=True, kv=True, end=False)
            part(0, 0, 0, now=True, nxt=True, kv=True, end=False)
            part(1, 0, 1, now=True, nxt=True, kv=True, end=True)
            with eng.Fori(1, B // 2 - 1) as i:
                for p in range(2):
                    part(2 * i + p, i, p, now=True, nxt=True, kv=True, end=True)
            part(B - 2, B // 2 - 1, 0, now=True, nxt=True, kv=False, end=True)
            part(B - 1, B // 2 - 1, 1, now=True, nxt=False, kv=False, end=True)
            part(B, B // 2, 0, now=False, nxt=False, kv=False, end=True)

        def included(now, nxt, kv, end):
            has = {"st": now, "pv": now, "u": nxt, "qb": nxt, "mx": nxt, "kv": kv, "last": end, "o": end}
            return [w for w in ORDER if (nxt if w == ("vt", 2) else kv if w[0] == "vt" else has[w[0]])]

        def wait_weights(eng, k):
            for n, (a, _) in enumerate(WP):
                if k == a:
                    eng.wait_ge(w_in[n], 16)

        @block.sync
        def _(sync):
            sync.dma_start(xnat, x_nat.rearrange("(n p) d -> p n d", p=128)).then_inc(x_in, 16)
            for dst, src in [(ident[:, :], c_ident), (identb[:, :], c_identb),
                             (wq[:, :, :], w_q.rearrange("(h p) n -> p h n", p=128)),
                             (wkv[:, :, :], w_kv.rearrange("(h p) n -> p h n", p=128)),
                             (wo[:, :, :], w_o), (gate[:, :, :], gate_w.rearrange("(h p) n -> p h n", p=128)),
                             (resid[:, :, :], x_tr.rearrange("(h p) t -> p h t", p=128))]:
                sync.dma_start(dst, src).then_inc(small_in, 16)
            for p in range(2):
                sync.dma_start(kvin[p][:, :, :], ctx_tr[p].rearrange("(h p) k -> p h k", p=128)) \
                    .then_inc(kvin_in[p], 16)
            sync.dma_start(maskin, mask).then_inc(mask_in, 16)
            for p in range(2):
                sync.dma_start(kst[p][EXTRA:MASKROW, :, :], c_krows).then_inc(rows_in, 16)
            sync.dma_start(qst[EXTRA:ROWS, :, :], c_qrows).then_inc(rows_in, 16)
            sync.wait_ge(mask_cut, 1)
            sync.dma_start(mask_bias, maskb).then_inc(mask_out, 16)
            sync.wait_ge(mask_out, 16)
            for m in range(2):
                sync.wait_ge(q_cut, 4 * NBLK * (m + 1))
                for band, part, n in [(0, 0, 3), (3, 1, 2), (5, 2, 1)]:
                    sync.dma_start(q_parts[m, band:band + n].rearrange("b r t -> r b t"),
                                   qparts[:, part:part + 1, :].to_broadcast([128, n, T])).then_inc(qw_done, 16)
                sync.wait_ge(qw_done, 48 * (m + 1))
                sync.dma_start(qst[0:BANDS, m * 8:m * 8 + 8, :],
                               q_parts[m].rearrange("b (d h) t -> (b d) h t", h=8)).then_inc(qst_in, 16)

            def part(b, i, p, now, nxt, kv, end):
                if nxt and kv:
                    sync.wait_ge(kv_ready, 3 * (b + 2))
                    load_ctx(b + 3, (p + 3) % 2)
                for t in range(3 if kv else 0):
                    k0, ks = THIRD[t]
                    k = 3 * (b + 2) + t
                    sync.wait_ge(k_cut, 3 * k + 3)
                    for band, m in [(0, 3), (3, 2), (5, 1)]:
                        if now and m == 1:
                            sync.wait_ge(st_ready, NC * b + 4 * t + 4)
                        sync.dma_start(k_parts[p, band:band + m, :, k0:k0 + ks].rearrange("b r k -> r b k"),
                                       kparts[(p + t) % 2][:, 0:m, 0:ks]).then_inc(kw_done, 16)
                    sync.wait_ge(kw_done, 48 * (k + 1))
                    sync.dma_start(kst[p][0:BANDS, :, k0:k0 + ks],
                                   k_parts[p, :, :, k0:k0 + ks].rearrange("b (d g) k -> (b d) g k", g=G)) \
                        .then_inc(kst_in[t], 16)
                    sync.dma_start(kst[p][MASKROW:ROWS, :, k0:k0 + ks],
                                   row(mask_bias, b + 2)[:, k0:k0 + ks].unsqueeze(1).to_broadcast([1, G, ks])) \
                        .then_inc(kst_in[t], 16)

            def row(a, r):
                return a[bass.ds(r, 1), :]

            def load_ctx(r, n):
                src = ctx_tr[bass.ds(r, 1)].rearrange("o (h p) k -> p (o h) k", p=128)
                sync.dma_start(kvin[n][:, :, :], src).then_inc(kvin_in[n], 16)

            over_batches(sync, part)

            sync.wait_ge(qs_done, B)
            sync.wait_ge(kv_ready, 3 * B)
            sync.wait_ge(kvin_in[0], 16 * (B // 2 + 1))
            sync.wait_ge(kvin_in[1], 16 * (B // 2))
            for n, (a, z) in enumerate(WP):
                sync.dma_start(wmoe[:, a:z], w_moe[:, a:z]).then_inc(w_in[n], 16)

            sync.wait_ge(norm_step, 4 * B)
            sync.dma_start(sel[:, :], c_sel).then_inc(sel_in, 16)
            with sync.Fori(0, NBLK) as t:
                sync.wait_ge(out_done, t + 1)
                sync.dma_start(out_tr.rearrange("(h p) t -> p h t", p=128)[:, :, bass.ds(t * BLK, BLK)],
                               resid[:, :, bass.ds(t * BLK, BLK)]).then_inc(out_sent, 16)
            sync.wait_ge(out_sent, 16 * NBLK)

        @block.tensor
        def _(pe):
            def turn(src, n, banks, ready, before, base):
                pe.wait_ge(before, base + 2 * n + 2)
                if n >= 2:
                    pe.wait_ge(xt_done, base // 2 + n - 1)
                for a in range(2):
                    for h in range(2):
                        mm = pe.transpose(banks[n % 2][:, h * 256 + a * 128:h * 256 + a * 128 + 128],
                                          src[:, 2 * n + a, h * 128:h * 128 + 128], ident[:, :])
                mm.then_inc(ready, 1)

            pe.wait_ge(small_in, 16 * 7)
            for n in range(NT // 2):
                turn(xnat, n, sbk, xt_ready, xn_done, 0)
            pe.wait_ge(xt_done, NT // 2)
            for m in range(2):
                for t in range(NBLK):
                    if m:
                        pe.wait_ge(q_out, NBLK * (m - 1) + t + 1)
                    for h in range(2):
                        mm = pe.matmul(qbank[t][:, 0:BLK], wq[:, h, m * 128:m * 128 + 128],
                                       xnT[:, h, bass.ds(t * BLK, BLK)], start=(h == 0), stop=(h == 1))
                    mm.then_inc(q_ready, 1)

            def scores(b, p, c):
                k0, ks = CHUNK[c]
                if c == 0:
                    pe.wait_ge(qmax_done, b + 1)
                pe.wait_ge(exp_done, NC * b + c - 1 + CREDIT)
                for g in range(G):
                    mm = pe.matmul(stp[c % 2][0:ks, g // 2, (g % 2) * 224:(g % 2) * 224 + 224],
                                   kst[p][:, g, k0:k0 + ks], qb[p][:, g * 224:g * 224 + 224], start=True, stop=True)
                mm.then_inc(st_ready, 1)

            def values(b, p, c):
                ks = CHUNK[c][1]
                if c == 0:
                    pe.wait_ge(o_done, b + 1)
                if c % 4 == 0:
                    pe.wait_ge(v_done, 4 * b + VSTEPS[c // 4])
                pe.wait_ge(exp_done, NC * b + c + 1 + CREDIT)
                for g in range(G):
                    mm = pe.matmul(obk[32 * g:32 * g + 32, 0:224], vaug[p][0:ks, c, g, :],
                                   probs[c % 2][0:ks, g * 224:g * 224 + 224], start=(c == 0), stop=(c == NC - 1))
                if c == NC - 1:
                    mm.then_inc(pv_ready, 1)

            def unit(b, n, u):
                t, q = divmod(u, 2 * G)
                k0, ks = THIRD[t]
                if q == 0:
                    pe.wait_ge(kst_in[t], 32 * (b + 1))
                if u == 0:
                    pe.wait_ge(qs_done, b + 1)
                if u >= 2 or not isinstance(b, int) or b > 0:
                    pe.wait_ge(max_done, NU * b + u - 1)
                pe.matmul(sbk[u % 2][0:TQ, 0:ks], qs[n][:, q * TQ:q * TQ + TQ],
                          kst[n][:, q // 2, k0:k0 + ks], start=True, stop=True).then_inc(s_ready, 1)

            def project(b, i, p, t, h):
                k0, ks = THIRD[t]
                if h == 0:
                    if not isinstance(b, int) or b or t:
                        pe.wait_ge(v_done, 4 * b + (VSTEPS[t - 1] if t else 0))
                    if t == 0:
                        pe.wait_ge(kvin_in[p], 16 * (i + 1))
                mm = pe.matmul(misc[:, 0:ks], wkv[:, h, :], kvin[p][:, h, k0:k0 + ks], start=(h == 0), stop=(h == 1))
                if h == 1:
                    mm.then_inc(kv_ready, 1)

            def turn_v(b, p, t):
                pe.wait_ge(kv_out, 2 * (3 * b + t) + 2)
                for a in range(4):
                    ks = CHUNK[4 * t + a][1]
                    mm = pe.transpose(misc[0:ks, a * 128:a * 128 + 128],
                                      kvf[(p + t) % 2][:, a * 128:a * 128 + ks], ident[:, :])
                mm.then_inc(vt_ready, 1)

            def turn_max(b):
                pe.wait_ge(nmax_step, 5 * (b + 1))
                for q in range(2 * G):
                    mm = pe.transpose(sbkb[EXTRA:EXTRA + 3, q * TQ:q * TQ + TQ], nparts[:, q, :],
                                      identb[0:TQ, 0:TQ])
                mm.then_inc(nmaxT_ready, 1)

            def part(b, i, p, now, nxt, kv, end):
                for w in included(now, nxt, kv, end):
                    if w[0] == "st":
                        scores(b, p, w[1])
                    elif w[0] == "pv":
                        values(b, p, w[1])
                    elif w[0] == "u":
                        unit(b + 1, (p + 1) % 2, w[1])
                    elif w[0] == "kv":
                        project(b + 2, i + 1, p, w[1], w[2])
                    elif w[0] == "vt" and w[1] == 2:
                        turn_v(b + 1, (p + 1) % 2, 2)
                    elif w[0] == "vt":
                        turn_v(b + 2, p, w[1])
                    elif w[0] == "mx":
                        turn_max(b + 1)
                    elif w[0] == "last":
                        values(b - 1, (p + 1) % 2, NC - 1)

            pe.wait_ge(q_out, 2 * NBLK)
            pe.wait_ge(rows_in, 48)
            over_batches(pe, part)

            for t in range(NBLK):
                pe.wait_ge(norm_step, 4 * B)
                if t >= 2:
                    pe.wait_ge(res_done, t - 1)
                for h in range(2):
                    for j in range(J):
                        mm = pe.matmul(stp[t % 2][:, h, 0:BLK], wo[:, j, h * 128:h * 128 + 128],
                                       attn[:, j, bass.ds(t * BLK, BLK)], start=(j == 0), stop=(j == J - 1))
                mm.then_inc(y_ready, 1)
            pe.wait_ge(res_done, NBLK)
            for n in range(NT // 2):
                if n >= 2:
                    pe.wait_ge(x1_done, n - 1)
                for a in range(2):
                    for h in range(2):
                        c0 = (2 * n + a) * 128
                        mm = pe.transpose(sbk[n % 2][:, a * 256 + h * 128:a * 256 + h * 128 + 128],
                                          resid[:, h, c0:c0 + 128], ident[:, :])
                mm.then_inc(x1t_ready, 1)
            pe.wait_ge(x1_done, NT // 2)
            for n in range(NT // 2):
                turn(x1nat, n, sbk, xt_ready, xn_done, NT)
            pe.wait_ge(xt_done, NT)
            for n in range(NT):
                for h in range(2):
                    mm = pe.matmul(misc[:, n * E:n * E + E], x2T[:, h, n * 128:n * 128 + 128], gate[:, h, :],
                                   start=(h == 0), stop=(h == 1))
            mm.then_inc(lg_ready, 1)
            pe.wait_ge(cp_done, 1)
            pe.wait_ge(score_done, 1)
            combT = [obk[:, :].bitcast(BF16), misc[:, :].bitcast(BF16)]
            for n in range(NT):
                mm = pe.transpose(combT[n // 8][0:3 * E, n % 8 * 128:n % 8 * 128 + 128], cparts[:, n, :], identb[:, :])
            mm.then_inc(ct_ready, 1)
            pe.wait_ge(ct_done, 2)
            pe.wait_ge(sel_in, 16)

            pe.wait_ge(x2_cut, NT // 2)
            PARTS = [(0, 0), (0, 1), (1, 0)]

            def down(s, k):
                pe.wait_ge(hid_step, 4 * s + 4)
                pe.wait_ge(d_cut[1], s + 1)
                for h in range(2):
                    for n, (a, z) in enumerate(PARTS):
                        mm = pe.matmul([obk, misc][h][:, 0:BLK], wdp[k % 2][a][:, h, :], hidp[k % 2][z][:, :],
                                       start=(k == 0 and n == 0), stop=(k == NH - 1 and n == 2))
                mm.then_inc(down_done, 1)

            def tiles(t, first):
                for k in range(NH):
                    s = NH * t + k
                    if not (first and k < 2):
                        pe.wait_ge(hid_step, 4 * (s - 2) + 2)
                    pe.wait_ge(gu_cut[1], s + 1)
                    for o in range(2):
                        for h in range(2):
                            for n, (a, z) in enumerate(PARTS):
                                pe.matmul(stp[k % 2][:, o, 0:BLK], wgup[k % 2][a][:, 2 * o + h, :],
                                          x2p[z][:, h, bass.ds(t * BLK, BLK)],
                                          start=(h == 0 and n == 0), stop=(h == 1 and n == 2))
                    pe.matmul(sbk[k % 2][:, 0:BLK], sel[:, k * 128:k * 128 + 128], combine[:, bass.ds(t * BLK, BLK)],
                              start=True, stop=True).then_inc(gu_ready, 1)
                    if k == 2 and not first:
                        pe.wait_ge(out_done, t)
                    if not (first and k < 2):
                        down(s - 2, (k - 2) % NH)

            tiles(0, True)
            with pe.Fori(1, NBLK) as t:
                tiles(t, False)
            for k in (NH - 2, NH - 1):
                down(NH * (NBLK - 1) + k, k)

        @block.scalar
        def _(act):
            act.wait_ge(ones_set, 1)
            for n in range(CREDIT):
                nc.scalar.activation(warm[:, n:n + 1], warm[:, n:n + 1], ACT.Exp).then_inc(exp_done, 1)
            act.wait_ge(var_done, 1)
            nc.scalar.activation(std[:, :], var[:, :], ACT.Sqrt).then_inc(std_done, 1)
            for n in range(NT // 2):
                act.wait_ge(xt_ready, n + 1)
                nc.scalar.copy(xnT[:, :, n * 256:n * 256 + 256],
                               sbk[n % 2][:, :].rearrange("p (h t) -> p h t", h=2)).then_inc(xt_done, 1)
            for k in range(2 * NBLK):
                act.wait_ge(q_ready, k + 1)
                if k >= 2:
                    act.wait_ge(q_cut, 4 * (k - 1))
                nc.scalar.mul(qf[k % 2][:, :], qbank[k % NBLK][:, 0:BLK], DH ** -0.5).then_inc(q_out, 1)

            def take_v(b, p, t):
                act.wait_ge(vt_ready, 3 * b + t + 1)
                for a, z, ks in ([(0, 4, 128)] if t < 2 else [(0, 3, 128), (3, 4, CHUNK[-1][1])]):
                    nc.scalar.copy(vaug[p][0:ks, 4 * t + a:4 * t + z, :, 0:DH],
                                          misc[0:ks, :].rearrange("k (c w g d) -> k c w g d", w=2, g=G, d=DH)
                                          [:, a:z, 1]).then_inc(v_done, 1)

            def part(b, i, p, now, nxt, kv, end):
                for w in included(now, nxt, kv, end):
                    if w[0] == "st":
                        c = w[1]
                        ks = CHUNK[c][1]
                        act.wait_ge(st_ready, NC * b + c + 1)
                        nc.scalar.activation(probs[c % 2][0:ks, :].rearrange("k (a n) -> k a n", a=2),
                                             stp[c % 2][0:ks, :, 0:448], ACT.Exp).then_inc(exp_done, 1)
                    elif w[0] == "vt" and w[1] == 2:
                        take_v(b + 1, (p + 1) % 2, 2)
                    elif w[0] == "vt":
                        take_v(b + 2, p, w[1])
                    elif w[0] == "kv" and w[2] == 1:
                        t = w[1]
                        k = 3 * (b + 2) + t
                        n = (p + t) % 2
                        ts = THIRD[t][1]
                        act.wait_ge(kv_ready, k + 1)
                        if not isinstance(k, int) or k >= 2:
                            act.wait_ge(vt_ready, k - 1)
                            act.wait_ge(k_cut, 3 * (k - 1))
                            act.wait_ge(kw_done, 48 * (k - 1))
                        nc.scalar.copy(kparts[n][:, 0, 0:ts], misc[0:64, 0:ts]).then_inc(kv_out, 1)
                        nc.scalar.copy(kvf[n][:, 0:ts], misc[:, 0:ts]).then_inc(kv_out, 1)

            act.wait_ge(ones_set, 4)
            over_batches(act, part)

            for n in range(NT // 2):
                act.wait_ge(x1t_ready, n + 1)
                nc.scalar.copy(x1nat[:, 2 * n:2 * n + 2, :],
                               sbk[n % 2][:, :].rearrange("p (a d) -> p a d", a=2)).then_inc(x1_done, 1)
            act.wait_ge(var_done, 2)
            nc.scalar.activation(std[:, :], var[:, :], ACT.Sqrt).then_inc(std_done, 1)
            for n in range(NT // 2):
                act.wait_ge(xt_ready, NT // 2 + n + 1)
                nc.scalar.copy(x2p[0][:, :, n * 256:n * 256 + 256],
                               sbk[n % 2][:, :].rearrange("p (h t) -> p h t", h=2)).then_inc(x2_high, 1)
                nc.scalar.copy(x2T[:, :, n * 256:n * 256 + 256],
                               sbk[n % 2][:, :].rearrange("p (h t) -> p h t", h=2)).then_inc(xt_done, 1)
            act.wait_ge(lg_ready, 1)
            nc.scalar.activation(score[:, :, 0:E], misc[:, 0:NT * E].rearrange("p (n e) -> p n e", e=E),
                                 ACT.Sigmoid).then_inc(score_done, 1)

            def cut_gu(k):
                nc.scalar.copy(wgup[k % 2][0][:, :, :], wmoe[:, k, 0:4, :]).then_inc(gu_cut[0], 1)

            def cut_d(k):
                nc.scalar.copy(wdp[k % 2][0][:, :, :], wmoe[:, k, 4:6, :]).then_inc(d_cut[0], 1)

            def tiles(t, first):
                for k in range(NH):
                    act.wait_ge(gu_ready, NH * t + k + 1)
                    nc.scalar.activation(silu[k % 2][:, :], stp[k % 2][:, 0, 0:BLK], ACT.Silu).then_inc(silu_done, 1)
                    if first:
                        wait_weights(act, k + 2)
                    cut_gu((k + 2) % NH)
                    if not (first and k == 0):
                        cut_d((k - 1) % NH)

            wait_weights(act, 0)
            cut_gu(0)
            cut_gu(1)
            tiles(0, True)
            with act.Fori(1, NBLK) as t:
                tiles(t, False)
            act.wait_ge(down_done, NH * NBLK - 2)
            cut_d(NH - 1)

        @block.gpsimd
        def _(pool):
            nc.gpsimd.memset(warm[:, :], 0.0).then_inc(ones_set, 1)
            nc.gpsimd.memset(zero[:, :], 0.0).then_inc(ones_set, 1)
            for n in range(2):
                nc.gpsimd.memset(vaug[n][:, :, :, DH:32], 1.0).then_inc(ones_set, 1)

            def part(b, i, p, now, nxt, kv, end):
                for t in range(3 if kv else 0):
                    k = 3 * (b + 2) + t
                    n = (p + t) % 2
                    ts = THIRD[t][1]
                    pool.wait_ge(kv_out, 2 * k + 2)
                    if not (isinstance(k, int) and k == 0):
                        pool.wait_ge(k_cut, 3 * k)
                    nc.gpsimd.tensor_tensor(kres[:, 0:ts], kvf[n][0:64, 0:ts], kparts[n][:, 0, 0:ts],
                                            ALU.subtract).then_inc(k_cut, 1)
                    nc.gpsimd.tensor_tensor(kparts[n][:, 1, 0:ts], kvf[n][0:64, 0:ts], kparts[n][:, 0, 0:ts],
                                            ALU.subtract).then_inc(k_cut, 1)
                    pool.wait_ge(k_cut, 3 * k + 2)
                    nc.gpsimd.tensor_tensor(kparts[n][:, 2, 0:ts], kres[:, 0:ts], kparts[n][:, 1, 0:ts],
                                            ALU.subtract).then_inc(k_cut, 1)
                    if t != 1:
                        continue
                    if now:
                        pool.wait_ge(st_ready, NC * b + 1)
                        pool.wait_ge(qb_done, b + 1)
                    pool.wait_ge(ones_set, 4)
                    pool.wait_ge(rows_in, 48)
                    pool.wait_ge(qst_in, 32)
                    q = qst[:, :, bass.ds((b + 2) * NQ, NQ)]
                    nc.gpsimd.tensor_tensor(qs[p][:, :].rearrange("r (h q) -> r h q", h=H), q,
                                            zero[:, :].unsqueeze(2).to_broadcast([ROWS, H, NQ]), ALU.add) \
                        .then_inc(qs_done, 1)

            over_batches(pool, part)

            for n in range(NT // 2):
                pool.wait_ge(xt_done, NT // 2 + n + 1)
                c = slice(n * 256, n * 256 + 256)
                nc.gpsimd.tensor_tensor(x2p[1][:, :, c], x2T[:, :, c], x2p[0][:, :, c], ALU.subtract) \
                    .then_inc(x2_cut, 1)

            def cut_gu(s, k):
                pool.wait_ge(gu_cut[0], s + 1)
                nc.gpsimd.tensor_tensor(wgup[k % 2][1][:, :, :], wmoe[:, k, 0:4, :], wgup[k % 2][0][:, :, :],
                                        ALU.subtract).then_inc(gu_cut[1], 1)

            def cut_d(s, k):
                pool.wait_ge(d_cut[0], s + 1)
                nc.gpsimd.tensor_tensor(wdp[k % 2][1][:, :, :], wmoe[:, k, 4:6, :], wdp[k % 2][0][:, :, :],
                                        ALU.subtract).then_inc(d_cut[1], 1)

            def tiles(t, first):
                for k in range(NH):
                    s = NH * t + k
                    if first:
                        wait_weights(pool, k + 2)
                    cut_gu(s + 2, (k + 2) % NH)
                    if not (first and k == 0):
                        cut_d(s - 1, (k - 1) % NH)

            wait_weights(pool, 0)
            cut_gu(0, 0)
            cut_gu(1, 1)
            tiles(0, True)
            with pool.Fori(1, NBLK) as t:
                tiles(t, False)
            cut_d(NH * NBLK - 1, NH - 1)

        @block.vector
        def _(dve):
            step = [0]

            def own(ins):
                ins.then_inc(vec, 1)
                step[0] += 1
                return step[0]

            dve.wait_ge(mask_in, 16)
            nc.vector.tensor_scalar(maskb, maskin, -1.0, -MASKED, ALU.add, ALU.mult) \
                .then_inc(mask_cut, 1)

            def layer_norm(x, turn):
                for n in range(NT):
                    last = own(nc.vector.bn_stats(stats[:, n, :], x[:, n, :]))
                dve.wait_ge(vec, last)
                for n in range(NT):
                    last = own(nc.vector.bn_aggr(mv[:, n, :], stats[:, n, :]))
                dve.wait_ge(vec, last)
                nc.vector.tensor_scalar(var[:, :], mv[:, :, 1], EPS, None, ALU.add).then_inc(var_done, 1)
                dve.wait_ge(std_done, turn)
                dve.wait_ge(vec, own(nc.vector.reciprocal(rstd[:, :], std[:, :])))
                dve.wait_ge(vec, own(nc.vector.tensor_tensor(newt[:, :], rstd[:, :], rstd[:, :], ALU.mult)))
                dve.wait_ge(vec, own(nc.vector.tensor_tensor(newt[:, :], newt[:, :], var[:, :], ALU.mult)))
                dve.wait_ge(vec, own(nc.vector.tensor_scalar(newt[:, :], newt[:, :], -0.5, 1.5, ALU.mult, ALU.add)))
                dve.wait_ge(vec, own(nc.vector.tensor_tensor(rstd[:, :], rstd[:, :], newt[:, :], ALU.mult)))
                for n in range(NT):
                    nc.vector.tensor_scalar(x[:, n, :], x[:, n, :], mv[:, n, 0:1], rstd[:, n:n + 1],
                                            ALU.subtract, ALU.mult).then_inc(xn_done, 1)

            dve.wait_ge(x_in, 16)
            layer_norm(xnat, 1)
            for k in range(2 * NBLK):
                m, t = divmod(k, NBLK)
                c = slice(t * BLK, t * BLK + BLK)
                dve.wait_ge(q_out, k + 1)
                if m and t == 0:
                    dve.wait_ge(qw_done, 48)
                nc.vector.tensor_copy(qparts[:, 0, c], qf[k % 2][:, :]).then_inc(q_cut, 1)
                dve.wait_ge(q_cut, 4 * k + 1)
                nc.vector.tensor_tensor(qres[:, :], qf[k % 2][:, :], qparts[:, 0, c], ALU.subtract).then_inc(q_cut, 1)
                dve.wait_ge(q_cut, 4 * k + 2)
                nc.vector.tensor_copy(qparts[:, 1, c], qres[:, :]).then_inc(q_cut, 1)
                dve.wait_ge(q_cut, 4 * k + 3)
                nc.vector.tensor_tensor(qparts[:, 2, c], qres[:, :], qparts[:, 1, c], ALU.subtract).then_inc(q_cut, 1)
                dve.wait_ge(q_cut, 4 * k + 4)
            nc.vector.memset(nmax[:, :], 0.0).then_inc(o_done, 1)
            dve.wait_ge(o_done, 1)

            def minus_max(b, p):
                dve.wait_ge(max_done, NU * (b + 1))
                nc.vector.tensor_reduce(nmax[:, :], maxp[:, :, :], AX_X, ALU.max, negate=True) \
                    .then_inc(nmax_step, 1)
                dve.wait_ge(nmax_step, 5 * b + 1)
                nc.vector.tensor_copy(nparts[:, :, 0], nmax[:, :]).then_inc(nmax_step, 1)
                dve.wait_ge(nmax_step, 5 * b + 2)
                nc.vector.tensor_tensor(nres[:, :], nmax[:, :], nparts[:, :, 0], ALU.subtract) \
                    .then_inc(nmax_step, 1)
                dve.wait_ge(nmax_step, 5 * b + 3)
                nc.vector.tensor_copy(nparts[:, :, 1], nres[:, :]).then_inc(nmax_step, 1)
                dve.wait_ge(nmax_step, 5 * b + 4)
                nc.vector.tensor_tensor(nparts[:, :, 2], nres[:, :], nparts[:, :, 1], ALU.subtract) \
                    .then_inc(nmax_step, 1)
                dve.wait_ge(nmaxT_ready, b + 1)
                dve.wait_ge(qb_done, b + 1)
                nc.vector.tensor_copy(qb[p][EXTRA:EXTRA + 3, :], sbkb[EXTRA:EXTRA + 3, 0:QH]) \
                    .then_inc(qmax_done, 1)

            def finish(b, n):
                if n == 0:
                    dve.wait_ge(pv_ready, b + 1)
                    nc.vector.tensor_copy(attn[:, :, bass.ds(b * NQ, NQ)],
                                          obk[:, 0:224].rearrange("p (j q) -> p j q", j=J)).then_inc(norm_step, 1)
                    nc.vector.stream_shuffle(ssum, obk[:, 0:224], UP).then_inc(o_done, 1)
                elif n < 3:
                    if n == 1:
                        dve.wait_ge(o_done, b + 2)
                    c = slice((n - 1) * 112, n * 112)
                    nc.vector.reciprocal(srec[:, c], ssum[:, c]).then_inc(norm_step, 1)
                else:
                    o = attn[:, :, bass.ds(b * NQ, NQ)]
                    dve.wait_ge(norm_step, 4 * b + 3)
                    nc.vector.tensor_tensor(o, o, srec.rearrange("p (j q) -> p j q", j=J), ALU.mult) \
                        .then_inc(norm_step, 1)

            def part(b, i, p, now, nxt, kv, end):
                bn = b + 1
                for w in included(now, nxt, kv, end):
                    if w[0] == "u":
                        t, q = divmod(w[1], 2 * G)
                        dve.wait_ge(s_ready, NU * bn + w[1] + 1)
                        nc.vector.tensor_reduce(maxp[:, q, t:t + 1], sbk[w[1] % 2][0:TQ, 0:THIRD[t][1]], AX_X,
                                                ALU.max).then_inc(max_done, 1)
                    elif w[0] == "qb":
                        dve.wait_ge(qs_done, bn + 1)
                        if now:
                            dve.wait_ge(st_ready, NC * b + 1)
                        nc.vector.tensor_copy(qb[(p + 1) % 2][:, :], qs[(p + 1) % 2][:, :]).then_inc(qb_done, 1)
                    elif w[0] == "mx":
                        minus_max(bn, (p + 1) % 2)
                    elif w[0] == "o":
                        finish(b - 1, w[1])

            over_batches(dve, part)

            for t in range(NBLK):
                dve.wait_ge(y_ready, t + 1)
                r = resid[:, :, bass.ds(t * BLK, BLK)]
                nc.vector.tensor_tensor(r, r, stp[t % 2][:, :, 0:BLK], ALU.add).then_inc(res_done, 1)
            dve.wait_ge(x1_done, NT // 2)
            layer_norm(x1nat, 2)

            own(nc.vector.memset(combine[3 * E:3 * E + 1, :], 1.0))
            dve.wait_ge(vec, own(nc.vector.memset(score[:, :, E:E + 2], 2.0)))
            dve.wait_ge(score_done, 1)
            for n in range(NT):
                last = own(nc.vector.max(top8[:, n, :], score[:, n, :]))
            dve.wait_ge(vec, last)
            for n in range(NT):
                last = own(nc.vector.match_replace(rest[:, n, :], top8[:, n, :], score[:, n, :], -1.0))
            own(nc.vector.tensor_reduce(wsum[:, :], top8[:, :, 2:8], AX_X, ALU.add))
            dve.wait_ge(vec, step[0])
            own(nc.vector.scalar_tensor_tensor(out=chosen[:, :, :], in0=rest[:, :, 0:E], scalar=0.0,
                                               in1=score[:, :, 0:E], op0=ALU.is_lt, op1=ALU.mult))
            dve.wait_ge(vec, own(nc.vector.tensor_scalar(wsum[:, :], wsum[:, :], 1e-20, None, ALU.add)))
            dve.wait_ge(vec, own(nc.vector.reciprocal(wrec[:, :], wsum[:, :])))
            dve.wait_ge(vec, own(nc.vector.tensor_tensor(chosen[:, :, :], chosen[:, :, :],
                                                         wrec[:, :].unsqueeze(2).to_broadcast([128, NT, E]), ALU.mult)))
            dve.wait_ge(vec, own(nc.vector.tensor_copy(cparts[:, :, 0:E], chosen[:, :, :])))
            dve.wait_ge(vec, own(nc.vector.tensor_tensor(cres[:, :, :], chosen[:, :, :], cparts[:, :, 0:E],
                                                         ALU.subtract)))
            dve.wait_ge(vec, own(nc.vector.tensor_copy(cparts[:, :, E:2 * E], cres[:, :, :])))
            nc.vector.tensor_tensor(cparts[:, :, 2 * E:3 * E], cres[:, :, :], cparts[:, :, E:2 * E], ALU.subtract) \
                .then_inc(cp_done, 1)
            dve.wait_ge(ct_ready, 1)
            for n, bank, w in [(0, obk, 1024), (1, misc, T - 1024)]:
                nc.vector.tensor_copy(combine[0:3 * E, n * 1024:n * 1024 + w],
                                      bank[:, :].bitcast(BF16)[0:3 * E, 0:w]).then_inc(ct_done, 1)
            dve.wait_ge(ct_done, 2)

            def output(t):
                dve.wait_ge(down_done, NH * (t + 1))
                for h in range(2):
                    r = resid[:, h, bass.ds(t * BLK, BLK)]
                    ins = nc.vector.tensor_tensor(r, r, [obk, misc][h][:, 0:BLK], ALU.add)
                    if h == 0:
                        ins.then_inc(vec, 1)
                ins.then_inc(out_done, 1)

            def tiles(t, first):
                for k in range(NH):
                    s = NH * t + k
                    dve.wait_ge(silu_done, s + 1)
                    nc.vector.tensor_tensor(gated[:, :], silu[k % 2][:, :], stp[k % 2][:, 1, 0:BLK],
                                            ALU.mult).then_inc(hid_step, 1)
                    dve.wait_ge(hid_step, 4 * s + 1)
                    nc.vector.tensor_tensor(hid[:, :], gated[:, :], sbk[k % 2][:, 0:BLK], ALU.mult) \
                        .then_inc(hid_step, 1)
                    if not (first and k < 2):
                        dve.wait_ge(down_done, s - 1)
                    dve.wait_ge(hid_step, 4 * s + 2)
                    nc.vector.tensor_copy(hidp[k % 2][0][:, :], hid[:, :]).then_inc(hid_step, 1)
                    dve.wait_ge(hid_step, 4 * s + 3)
                    nc.vector.tensor_tensor(hidp[k % 2][1][:, :], hid[:, :], hidp[k % 2][0][:, :],
                                            ALU.subtract).then_inc(hid_step, 1)
                    if k == 1 and not first:
                        output(t - 1)

            tiles(0, True)
            with dve.Fori(1, NBLK) as t:
                tiles(t, False)
            output(NBLK - 1)


NP_BF16 = np.dtype(mybir.dt.np(BF16))


def _bf16_parts(a):
    a = np.asarray(a, np.float64)
    parts = []
    for _ in range(3):
        h = a.astype(NP_BF16)
        parts.append(h)
        a = a - h.astype(np.float64)
    return parts


def _constants():
    bf = NP_BF16
    slope = (np.float32(2.0 ** (-8.0 / H)) ** np.arange(1, H + 1, dtype=np.float32)).astype(np.float32)
    slope_parts = _bf16_parts(slope)
    q = np.arange(NQ, dtype=np.float64)
    shift_parts = _bf16_parts(-(slope.astype(np.float64)[:, None] * q[None, :]))
    qrows = np.zeros((ROWS - EXTRA, H, B, NQ), bf)
    for n in range(3):
        qrows[3 + n] = shift_parts[n][:, None, :]
        qrows[6 + n] = slope_parts[n][:, None, None]
        qrows[9 + n] = slope_parts[n][:, None, None]
    qrows[12] = 1.0
    keys = np.arange(NK)
    krows = np.zeros((12, G, NK), bf)
    krows[0:6] = 1.0
    krows[6:9] = (keys // 8 * 8).astype(np.float32)
    krows[9:12] = (keys % 8).astype(np.float32)
    sel = np.zeros((3 * E + 1, HP), bf)
    for e in range(E):
        for n in range(3):
            sel[n * E + e, e * FE:(e + 1) * FE] = 1.0
    sel[3 * E, E * FE:HID] = 1.0
    return {"c_ident": np.eye(128, dtype=np.float32), "c_identb": np.eye(128, dtype=np.float32).astype(bf),
            "c_krows": krows, "c_qrows": qrows.reshape(ROWS - EXTRA, H, T), "c_sel": sel}


def kernel(x, ctx_2048, mask_BxS2_bf1, L0_xattn_Wq, L0_xattn_Wk, L0_xattn_Wv, L0_xattn_Wo, L0_ffn_gate_w,
           L0_ffn_wg, L0_ffn_wu, L0_ffn_wd, L0_ffn_sg, L0_ffn_su, L0_ffn_sd):
    import concourse.bacc as bacc
    from concourse.bass_utils import run_bass_kernel_spmd

    def f(a):
        return np.asarray(a)

    def wide(routed, shared):
        a = np.concatenate([f(routed).transpose(1, 0, 2).reshape(D, E * FE), f(shared)], 1)
        return np.pad(a, ((0, 0), (0, HP - HID)))

    x2 = f(x).reshape(T, D)
    wq = f(L0_xattn_Wq).reshape(D, 2, 8, DH).transpose(0, 1, 3, 2).reshape(D, D)
    wk = f(L0_xattn_Wk).reshape(D, G, DH).transpose(0, 2, 1).reshape(D, G * DH)
    wo = np.pad(f(L0_xattn_Wo).reshape(G, J, DH, D).transpose(0, 2, 1, 3), ((0, 0), (0, DH), (0, 0), (0, 0)))
    gate_up = np.stack([wide(L0_ffn_wg, L0_ffn_sg), wide(L0_ffn_wu, L0_ffn_su)])
    down = np.pad(np.concatenate([f(L0_ffn_wd).reshape(E * FE, D), f(L0_ffn_sd)], 0), ((0, HP - HID), (0, 0)))
    arrays = {
        "x_nat": x2,
        "x_tr": x2.T,
        "ctx_tr": np.pad(f(ctx_2048).transpose(0, 2, 1), ((0, 1), (0, 0), (0, 0))),
        "mask": f(mask_BxS2_bf1).view(np.uint8),
        "w_q": wq,
        "w_kv": np.concatenate([wk, f(L0_xattn_Wv)], 1),
        "w_o": wo.reshape(128, J, D),
        "gate_w": f(L0_ffn_gate_w),
        "w_moe": np.stack([*gate_up.reshape(4, 128, NH, 128), *down.reshape(NH, 128, 2, 128).transpose(2, 1, 0, 3)],
                          2),
        **_constants(),
    }
    arrays = {n: np.ascontiguousarray(a) for n, a in arrays.items()}
    nc = bacc.Bacc("TRN2", target_bir_lowering=False, num_devices=1)
    aps = [_dram_in(nc, n, a.shape, mybir.dt.from_np(a.dtype)) for n, a in arrays.items()]
    out = nc.dram_tensor("out_tr", (D, T), F32, kind="ExternalOutput").ap()
    build(nc, *aps, out)
    r = run_bass_kernel_spmd(nc, [arrays], core_ids=[0])
    return np.ascontiguousarray(r.results[0]["out_tr"].T).reshape(B, NQ, D)
```

```python
from contextlib import ExitStack

import numpy as np

import concourse.bass as bass
from concourse import mybir

F32 = mybir.dt.float32
BF16 = mybir.dt.bfloat16
U8 = mybir.dt.uint8
F32R = mybir.dt.float32r
ALU = mybir.AluOpType
ACT = mybir.ActivationFunctionType
AX_X = mybir.AxisListType.X

B, NQ, D = 32, 56, 256
NK = 1500
G, J, DH = 4, 4, 16
H = G * J
T = B * NQ
NT = T // 128
BLK = 448
NBLK = T // BLK
TM = BLK // 4
NM = T // TM
E, TOPK, FE, FS = 32, 6, 96, 192
HID = E * FE + FS
NH = -(-HID // 128)
HP = NH * 128
EPS = 1e-5

THIRD = [(0, 512), (512, 512), (1024, NK - 1024)]
CHUNK = [(c, min(128, NK - c)) for c in range(0, NK, 128)]
NC = len(CHUNK)
QH = H * NQ
TQ = 2 * NQ
NU = 3 * 2 * G


def batch_order():
    cost = {"st": 36, "pv": 41, "kv": 64, "vt": 22, "last": 41, "mx": 15, "qb": 0, "o": 0, "cx": 0}
    work = []
    for c in range(NC):
        if c == NC - 1:
            work.append(("mx",))
        work.append(("st", c))
        if c == 0:
            work += [("last",), ("o", 0), ("vt", 2)]
        if c in END_STEPS:
            work.append(("o", END_STEPS.index(c) + 1))
        if c == COPY_STEP:
            work.append(("qb",))
        if c in KV_STEPS:
            work.append(("kv", KV_STEPS.index(c), 0))
        if c:
            work.append(("pv", c - 1))
        if c in KV_STEPS:
            work.append(("kv", KV_STEPS.index(c), 1))
        if c + 1 in KV_STEPS:
            work.append(("cx", KV_STEPS.index(c + 1)))
        if c in (4, 8):
            work.append(("vt", c // 4 - 1))
    last = sum(cost[w[0]] for w in work) - UNITS_END
    order, done, n = [], 0, 0
    for w in work:
        order.append(w)
        done += cost[w[0]]
        burst = 0
        while n < NU and burst < UNITS_BURST and done >= UNITS_BEGIN + (last - UNITS_BEGIN) * n / (NU - 1):
            order.append(("u", n))
            n += 1
            burst += 1
    assert n == NU
    return order


UNITS_BEGIN, UNITS_END, UNITS_BURST = 80, 300, 2
KV_STEPS = (2, 6, 10)
END_STEPS, COPY_STEP = (2, 3, 4), 5

ORDER = batch_order()

QBANDS = [0, 0, 0, 1, 1, 2]
NBAND = len(QBANDS)
BANDS = NBAND * DH
EXTRA = BANDS
MASKROW = EXTRA + 12
ROWS = MASKROW + 1
MASKED = -2.0 ** 100

PARTS = [(0, 0), (0, 1), (1, 0)]

VSTEPS = [1, 2, 4]
UP = list(range(16, 32)) * 2
CREDIT = 2


def _dram_in(nc, name, shape, dt):
    return nc.dram_tensor(name, shape, dt, kind="ExternalInput").ap()


def build(nc, x_nat, x_tr, ctx_tr, mask, w_q, w_kv, w_o, gate_w, w_moe, c_ident, c_identb, c_krows,
          c_qrows, c_sel, out_tr):
    ctx = ExitStack()
    with ctx:
        def sb(name, shape, dt, scope=ctx):
            return scope.enter_context(nc.sbuf_tensor(name, shape, dt))

        def sem(name):
            return ctx.enter_context(nc.semaphore(name))

        ident = sb("ident", [128, 128], F32)
        identb = sb("identb", [128, 128], BF16)
        wq = sb("wq", [128, 2, D], F32)
        wkv = sb("wkv", [128, 2, 128], F32)
        wo = sb("wo", [128, J, D], F32)
        gate = sb("gate", [128, 2, E], F32)
        attn_scope = ExitStack()
        attn = sb("attn", [128, J, T], F32, attn_scope)
        attn_scope.close()
        x2parts = sb("x2parts", [128, 4, T], F32R)
        x2p = [x2parts[:, 0:2, :], x2parts[:, 2:4, :]]
        stats = sb("stats", [128, NM, 6], F32)
        mv = sb("mv", [128, NM, 2], F32)
        var = sb("var", [128, NM], F32)
        std = sb("std", [128, NM], F32)
        rstd = sb("rstd", [128, NM], F32)
        newt = sb("newt", [128, NM], F32)
        warm = sb("warm", [1, 2], F32)

        att = ExitStack()
        qst = sb("qst", [ROWS, H, T], BF16, att)
        kvin = [sb(f"kvin{p}", [128, 2, NK], F32, att) for p in range(2)]
        kst0 = sb("kst0", [ROWS, G, NK], BF16, att)
        cxp = [[sb(f"cxp{p}{a}", [128, 2, 512], F32R, att) for a in range(2)] for p in range(2)]
        wkvp = [sb(f"wkvp{a}", [128, 2, 128], F32R, att) for a in range(2)]
        early = ExitStack()
        qparts0 = sb("qparts0", [128, 3, T], BF16, early)
        early.close()
        kst = [kst0, sb("kst1", [ROWS, G, NK], BF16, att)]
        kvf = [sb(f"kvf{p}", [128, 512], F32, att) for p in range(2)]
        kparts = [sb(f"kparts{p}", [64, 3, 512], BF16, att) for p in range(2)]
        kres = sb("kres", [64, 512], F32, att)
        vaug = [sb(f"vaug{p}", [128, NC, G, 32], F32, att) for p in range(2)]
        probs = [sb(f"probs{p}", [128, QH], F32, att) for p in range(2)]
        qs = [sb(f"qs{p}", [ROWS, QH], BF16, att) for p in range(2)]
        qb = [sb(f"qb{p}", [ROWS, QH], BF16, att) for p in range(2)]
        alive = sb("alive", [ROWS, B], F32, att)
        some = sb("some", [B, 1], F32, att)
        maxp = sb("maxp", [TQ, 2 * G, 3], F32, att)
        nmax = sb("nmax", [TQ, 2 * G], F32, att)
        nres = sb("nres", [TQ, 2 * G], F32, att)
        nparts = sb("nparts", [TQ, 2 * G, 3], BF16, att)
        maskin = probs[0][:, :].bitcast(U8)[0:B, 0:NK]
        maskb = probs[1][:, :].bitcast(BF16)[0:B, 0:NK]
        qf = [sb(f"qf{p}", [128, BLK], F32, att) for p in range(2)]
        qres = sb("qres", [128, BLK], F32, att)
        ssum, srec = (qf[p][:, 0:224] for p in range(2))
        attn_flat = attn[:, :, :].rearrange("p j t -> p (j t)")
        xnat = attn_flat[:, 0:NT * D].rearrange("p (n d) -> p n d", d=D)
        xnT = attn_flat[:, NT * D:NT * D + 2 * T].rearrange("p (h t) -> p h t", h=2)
        qparts = [qparts0[:, :, :],
                  attn_flat[:, 0:3 * T // 2].bitcast(BF16).rearrange("p (n t) -> p n t", n=3)]
        att.close()

        wmoe = sb("wmoe", [128, NH, 6, 128], F32)
        assert NH * 6 * 128 * 4 <= H * T * 2 + 2 * 2 * NK * 4
        resid = sb("resid", [128, 2, T], F32)
        assert NH * 6 * 128 * 4 + 2 * T * 4 <= H * T * 2 + 2 * 2 * NK * 4 + G * NK * 2 + 2 * 512 * 4
        x1nat = sb("x1nat", [TM, NM, D], F32)
        x2T = [sb(f"x2T{p}", [128, 2, BLK], F32) for p in range(2)]
        score = sb("score", [TM, NM, E + 2], F32)
        top8 = sb("top8", [TM, NM, 8], F32)
        rest = sb("rest", [TM, NM, E + 2], F32)
        chosen = sb("chosen", [TM, NM, E], F32)
        wsum = sb("wsum", [TM, NM], F32)
        wrec = sb("wrec", [TM, NM], F32)
        share = sb("share", [TM, NM, E], F32)
        cres = sb("cres", [TM, NM, E], F32)
        cparts = sb("cparts", [TM, NM, 3 * E], BF16)
        combine = sb("combine", [3 * E + 1, T], BF16)
        sel = sb("sel", [3 * E + 1, HP], BF16)
        silu = [sb(f"silu{p}", [128, BLK], F32) for p in range(2)]
        gated = sb("gated", [128, BLK], F32)
        hid = sb("hid", [128, BLK], F32)
        hidp = [[sb(f"hidp{p}{a}", [128, BLK], F32R) for a in range(2)] for p in range(2)]
        wgup = [[sb(f"wgup{p}{a}", [128, 4, 128], F32R) for a in range(2)] for p in range(2)]
        wdp = [[sb(f"wdp{p}{a}", [128, 2, 128], F32R) for a in range(2)] for p in range(2)]

        stp = [ctx.enter_context(nc.psum_tensor(f"stp{p}", [128, 2, 512], F32)) for p in range(2)]
        sbk = [ctx.enter_context(nc.psum_tensor(f"sbk{p}", [128, 512], F32)) for p in range(2)]
        obk = ctx.enter_context(nc.psum_tensor("obk", [128, 512], F32))
        misc = ctx.enter_context(nc.psum_tensor("misc", [128, 512], F32))
        sbkb = sbk[0][:, :].bitcast(BF16)
        qbank = [stp[0][:, 0, :], stp[0][:, 1, :], stp[1][:, 0, :], stp[1][:, 1, :]]

        k_parts = nc.dram_tensor("k_parts", (2, 3, DH * G, NK), BF16, kind="Internal").ap()
        q_parts = nc.dram_tensor("q_parts", (2, 128, 3, T), BF16, kind="Internal").ap()
        mask_bias = nc.dram_tensor("mask_bias", (B, NK), BF16, kind="Internal").ap()
        alive_row = nc.dram_tensor("alive_row", (B, 1), F32, kind="Internal").ap()

        x_in = sem("x_in")
        wkv_in = sem("wkv_in")
        wq_in = sem("wq_in")
        small_in = sem("small_in")
        resid_in = sem("resid_in")
        mask_in = sem("mask_in")
        rows_in = sem("rows_in")
        mask_cut = sem("mask_cut")
        mask_out = sem("mask_out")
        alive_in = sem("alive_in")
        ones_set = sem("ones_set")
        vec = sem("vec")
        var_done = sem("var_done")
        std_done = sem("std_done")
        xn_done = sem("xn_done")
        xt_ready = sem("xt_ready")
        xt_done = sem("xt_done")
        q_ready = sem("q_ready")
        q_out = sem("q_out")
        q_cut = sem("q_cut")
        qw_done = sem("qw_done")
        qst_in = sem("qst_in")
        kvin_in = [sem("kvin_in0"), sem("kvin_in1")]
        wkv_cut = [sem("wkv_high"), sem("wkv_low")]
        cx_cut = [sem("cx_high"), sem("cx_low")]
        kv_ready = sem("kv_ready")
        kv_out = sem("kv_out")
        k_cut = sem("k_cut")
        kw_done = sem("kw_done")
        kst_in = [[sem(f"kst_in{p}{t}") for t in range(3)] for p in range(2)]
        vt_ready = sem("vt_ready")
        v_done = sem("v_done")
        s_ready = sem("s_ready")
        max_done = sem("max_done")
        nmax_step = sem("nmax_step")
        nmaxT_ready = sem("nmaxT_ready")
        qs_done = sem("qs_done")
        qb_done = sem("qb_done")
        qmax_done = sem("qmax_done")
        st_ready = sem("st_ready")
        exp_done = sem("exp_done")
        pv_ready = sem("pv_ready")
        o_done = sem("o_done")
        norm_step = sem("norm_step")
        y_ready = sem("y_ready")
        res_done = sem("res_done")
        x1t_ready = sem("x1t_ready")
        x1_done = sem("x1_done")
        x2n_done = sem("x2n_done")
        x2t_ready = sem("x2t_ready")
        x2_high = sem("x2_high")
        x2T_done = sem("x2T_done")
        x2_cut = sem("x2_cut")
        lg_ready = sem("lg_ready")
        score_done = sem("score_done")
        chosen_done = sem("chosen_done")
        cp_step = sem("cp_step")
        cp_last = sem("cp_last")
        ct_ready = sem("ct_ready")
        ct_done = sem("ct_done")
        sel_in = sem("sel_in")
        NWP = 4
        WP = [(n * NH // NWP, (n + 1) * NH // NWP) for n in range(NWP)]
        w_in = [sem(f"w_in{n}") for n in range(NWP)]
        gu_ready = sem("gu_ready")
        gu_cut = [sem("gu_high"), sem("gu_low")]
        d_cut = [sem("d_high"), sem("d_low")]
        silu_done = sem("silu_done")
        hid_step = sem("hid_step")
        down_done = sem("down_done")
        out_done = sem("out_done")
        out_sent = sem("out_sent")

        block = ctx.enter_context(nc.Block())

        def first_batch(part):
            part(-2, -1, 0, kv=True)

        def over_batches(eng, part):
            part(-1, -1, 1, kv=True, turn=True)
            part(-1, -1, 1, nxt=True)
            part(0, 0, 0, now=True, nxt=True, turn=True, kv=True)
            part(1, 0, 1, now=True, nxt=True, turn=True, kv=True, end=True)
            with eng.Fori(1, B // 2 - 1) as i:
                for p in range(2):
                    part(2 * i + p, i, p, now=True, nxt=True, turn=True, kv=True, end=True)
            part(B - 2, B // 2 - 1, 0, now=True, nxt=True, turn=True, end=True)
            part(B - 1, B // 2 - 1, 1, now=True, end=True)
            part(B, B // 2, 0, end=True)

        def included(now, nxt, turn, kv, end):
            has = {"st": now, "pv": now, "u": nxt, "qb": nxt, "mx": nxt, "kv": kv, "cx": kv, "last": end, "o": end}
            return [w for w in ORDER if (turn if w == ("vt", 2) else kv if w[0] == "vt" else has[w[0]])]

        def turned_shares(t):
            bank = [stp[1][:, 1, :], stp[0][:, 0, :], sbk[0][:, :], sbk[1][:, :]][t]
            return bank.bitcast(BF16)[0:3 * E, 0:BLK]

        def wait_weights(eng, k):
            for n, (a, _) in enumerate(WP):
                if k == a:
                    eng.wait_ge(w_in[n], 16)

        def after(b, i, p, t):
            n = (t + 1) % 3
            k0, ks = THIRD[n]
            if n:
                return 3 * (b + 2) + n, kvin[p][:, :, k0:k0 + ks], cxp[(p + n) % 2], ks, None
            q = (p + 1) % 2
            return 3 * (b + 3), kvin[q][:, :, k0:k0 + ks], cxp[q], ks, (kvin_in[q], 16 * (i + 2 + p))

        @block.sync
        def _(sync):
            def load_kvin(p):
                sync.dma_start(kvin[p][:, :, :], ctx_tr[p].rearrange("(h p) k -> p h k", p=128)) \
                    .then_inc(kvin_in[p], 16)

            sync.dma_start(maskin, mask).then_inc(mask_in, 16)
            sync.dma_start(xnat, x_nat.rearrange("(n p) d -> p n d", p=128)).then_inc(x_in, 16)
            sync.dma_start(ident[:, :], c_ident).then_inc(wkv_in, 16)
            sync.dma_start(wkv[:, :, :], w_kv.rearrange("(h p) n -> p h n", p=128)).then_inc(wkv_in, 16)
            load_kvin(0)
            sync.dma_start(wq[:, :, :], w_q.rearrange("(h p) n -> p h n", p=128)).then_inc(wq_in, 16)
            sync.dma_start(kst[0][EXTRA:MASKROW, :, :], c_krows).then_inc(rows_in, 16)
            load_kvin(1)
            sync.dma_start(qst[EXTRA:ROWS, :, :], c_qrows).then_inc(rows_in, 16)
            for dst, src in [(identb[:, :], c_identb), (wo[:, :, :], w_o),
                             (gate[:, :, :], gate_w.rearrange("(h p) n -> p h n", p=128))]:
                sync.dma_start(dst, src).then_inc(small_in, 16)
            sync.wait_ge(mask_cut, 3)
            sync.dma_start(mask_bias, maskb).then_inc(mask_out, 16)
            sync.dma_start(alive_row, some[:, :]).then_inc(mask_out, 16)
            sync.wait_ge(mask_out, 32)
            sync.wait_ge(ones_set, 2)
            sync.dma_start(alive[0:MASKROW, :], alive_row.rearrange("b o -> o b").to_broadcast([MASKROW, B])) \
                .then_inc(alive_in, 16)
            def part(b, i, p, now=False, nxt=False, turn=False, kv=False, end=False):
                if now and kv:
                    load_ctx(b + 3, (p + 3) % 2)
                for t in range(3 if kv else 0):
                    k0, ks = THIRD[t]
                    k = 3 * (b + 2) + t
                    if isinstance(b, int) and b == -2 and t == 2:
                        load_ctx(2, 0)
                    sync.wait_ge(k_cut, 3 * k + 3)
                    for a, z in [(0, 1), (1, 3)]:
                        if now and a == 1:
                            sync.wait_ge(st_ready, NC * b + 4 * t + 4)
                        sync.dma_start(k_parts[p, a:z, :, k0:k0 + ks].rearrange("n r k -> r n k"),
                                       kparts[(p + t) % 2][:, a:z, 0:ks]).then_inc(kw_done, 16)
                    sync.wait_ge(kw_done, 32 * (k + 1))
                    for band, m in [(0, 3), (3, 2), (5, 1)]:
                        sync.dma_start(kst[p][band * DH:(band + m) * DH, :, k0:k0 + ks],
                                       k_parts[p, 0:m, :, k0:k0 + ks].rearrange("n (d g) k -> (n d) g k", g=G)) \
                            .then_inc(kst_in[p][t], 16)
                    sync.dma_start(kst[p][MASKROW:ROWS, :, k0:k0 + ks],
                                   row(mask_bias, b + 2)[:, k0:k0 + ks].unsqueeze(1).to_broadcast([1, G, ks])) \
                        .then_inc(kst_in[p][t], 16)

            def row(a, r):
                return a[bass.ds(r, 1), :]

            def load_ctx(r, n):
                sync.wait_ge(cx_cut[1], 3 * (r - 1))
                src = ctx_tr[bass.ds(r, 1)].rearrange("o (h p) k -> p (o h) k", p=128)
                sync.dma_start(kvin[n][:, :, :], src).then_inc(kvin_in[n], 16)

            first_batch(part)

            for m in range(2):
                sync.wait_ge(q_cut, 3 * NBLK * (m + 1))
                sync.dma_start(q_parts[m], qparts[m]).then_inc(qw_done, 16)
                sync.wait_ge(qw_done, 16 * (m + 1))
                if m == 1:
                    sync.dma_start(kst[1][EXTRA:MASKROW, :, :], c_krows).then_inc(rows_in, 16)
                for band, n in enumerate(QBANDS):
                    sync.dma_start(qst[band * DH:band * DH + DH, m * 8:m * 8 + 8, :],
                                   q_parts[m, :, n].rearrange("(d h) t -> d h t", h=8)).then_inc(qst_in, 16)
            over_batches(sync, part)

            sync.wait_ge(qs_done, B)
            sync.wait_ge(cx_cut[1], 3 * B + 1)
            sync.wait_ge(kvin_in[0], 16 * (B // 2 + 1))
            sync.wait_ge(kvin_in[1], 16 * (B // 2))
            for n, (a, z) in enumerate(WP):
                sync.dma_start(wmoe[:, a:z], w_moe[:, a:z]).then_inc(w_in[n], 16)

            sync.wait_ge(kv_ready, 3 * B)
            sync.wait_ge(st_ready, NC * (B - 1))
            sync.wait_ge(cx_cut[1], 3 * B + 1)
            sync.dma_start(resid[:, :, :], x_tr.rearrange("(h p) t -> p h t", p=128)).then_inc(resid_in, 16)

            sync.wait_ge(norm_step, 4 * B)
            sync.dma_start(sel[:, :], c_sel).then_inc(sel_in, 16)
            with sync.Fori(0, NBLK) as t:
                sync.wait_ge(out_done, t + 1)
                sync.dma_start(out_tr.rearrange("(h p) t -> p h t", p=128)[:, :, bass.ds(t * BLK, BLK)],
                               resid[:, :, bass.ds(t * BLK, BLK)]).then_inc(out_sent, 16)
            sync.wait_ge(out_sent, 16 * NBLK)

        @block.tensor
        def _(pe):
            def turn(src, n, banks, ready, before, base):
                pe.wait_ge(before, base + 2 * n + 2)
                if n >= 2:
                    pe.wait_ge(xt_done, base // 2 + n - 1)
                for a in range(2):
                    for h in range(2):
                        mm = pe.transpose(banks[n % 2][:, h * 256 + a * 128:h * 256 + a * 128 + 128],
                                          src[:, 2 * n + a, h * 128:h * 128 + 128], ident[:, :])
                mm.then_inc(ready, 1)

            def scores(b, p, c):
                k0, ks = CHUNK[c]
                if c == 0:
                    pe.wait_ge(qmax_done, b + 1)
                pe.wait_ge(exp_done, NC * b + c - 1 + CREDIT)
                for g in range(G):
                    mm = pe.matmul(stp[c % 2][0:ks, g // 2, (g % 2) * 224:(g % 2) * 224 + 224],
                                   kst[p][:, g, k0:k0 + ks], qb[p][:, g * 224:g * 224 + 224], start=True, stop=True)
                mm.then_inc(st_ready, 1)

            def values(b, p, c):
                ks = CHUNK[c][1]
                if c == 0:
                    pe.wait_ge(o_done, b + 1)
                if c % 4 == 0:
                    pe.wait_ge(v_done, 4 * b + VSTEPS[c // 4])
                pe.wait_ge(exp_done, NC * b + c + 1 + CREDIT)
                for g in range(G):
                    mm = pe.matmul(obk[32 * g:32 * g + 32, 0:224], vaug[p][0:ks, c, g, :],
                                   probs[c % 2][0:ks, g * 224:g * 224 + 224], start=(c == 0), stop=(c == NC - 1))
                if c == NC - 1:
                    mm.then_inc(pv_ready, 1)

            def unit(b, i, n, u):
                t, q = divmod(u, 2 * G)
                k0, ks = THIRD[t]
                if q == 0:
                    pe.wait_ge(kst_in[n][t], 64 * (i + 1))
                if u == 0:
                    pe.wait_ge(qs_done, b + 1)
                if u >= 2 or not isinstance(b, int) or b > 0:
                    pe.wait_ge(max_done, NU * b + u - 1)
                pe.matmul(sbk[u % 2][0:TQ, 0:ks], qs[n][:, q * TQ:q * TQ + TQ],
                          kst[n][:, q // 2, k0:k0 + ks], start=True, stop=True).then_inc(s_ready, 1)

            def project(b, p, t, h):
                k0, ks = THIRD[t]
                if h == 0:
                    if not isinstance(b, int) or b or t:
                        pe.wait_ge(v_done, 4 * b + (VSTEPS[t - 1] if t else 0))
                    pe.wait_ge(cx_cut[1], 3 * b + t + 1)
                for n, (a, z) in enumerate(PARTS):
                    mm = pe.matmul(misc[:, 0:ks], wkvp[a][:, h, :], cxp[(p + t) % 2][z][:, h, 0:ks],
                                   start=(h == 0 and n == 0), stop=(h == 1 and n == 2))
                if h == 1:
                    mm.then_inc(kv_ready, 1)

            def turn_v(b, p, t):
                pe.wait_ge(kv_out, 2 * (3 * b + t) + 2)
                for a in range(4):
                    ks = CHUNK[4 * t + a][1]
                    mm = pe.transpose(misc[0:ks, a * 128:a * 128 + 128],
                                      kvf[(p + t) % 2][:, a * 128:a * 128 + ks], ident[:, :])
                mm.then_inc(vt_ready, 1)

            def turn_max(b):
                pe.wait_ge(nmax_step, 5 * (b + 1))
                for q in range(2 * G):
                    mm = pe.transpose(sbkb[EXTRA:EXTRA + 3, q * TQ:q * TQ + TQ], nparts[:, q, :],
                                      identb[0:TQ, 0:TQ])
                mm.then_inc(nmaxT_ready, 1)

            def part(b, i, p, now=False, nxt=False, turn=False, kv=False, end=False):
                if nxt and not now:
                    pe.wait_ge(rows_in, 48)
                for w in included(now, nxt, turn, kv, end):
                    if w[0] == "st":
                        scores(b, p, w[1])
                    elif w[0] == "pv":
                        values(b, p, w[1])
                    elif w[0] == "u":
                        unit(b + 1, i + p, (p + 1) % 2, w[1])
                    elif w[0] == "kv":
                        project(b + 2, p, w[1], w[2])
                    elif w[0] == "vt" and w[1] == 2:
                        turn_v(b + 1, (p + 1) % 2, 2)
                    elif w[0] == "vt":
                        turn_v(b + 2, p, w[1])
                    elif w[0] == "mx":
                        turn_max(b + 1)
                    elif w[0] == "last":
                        values(b - 1, (p + 1) % 2, NC - 1)

            pe.wait_ge(wkv_in, 32)
            pe.wait_ge(wkv_cut[1], 1)
            first_batch(part)

            for n in range(NT // 2):
                turn(xnat, n, sbk, xt_ready, xn_done, 0)
            pe.wait_ge(xt_done, NT // 2)
            pe.wait_ge(wq_in, 16)
            for m in range(2):
                for t in range(NBLK):
                    if m:
                        pe.wait_ge(q_out, 2 * (NBLK * (m - 1) + t + 1))
                    for h in range(2):
                        mm = pe.matmul(qbank[t][:, 0:BLK], wq[:, h, m * 128:m * 128 + 128],
                                       xnT[:, h, bass.ds(t * BLK, BLK)], start=(h == 0), stop=(h == 1))
                    mm.then_inc(q_ready, 1)

            pe.wait_ge(q_out, 4 * NBLK)
            pe.wait_ge(small_in, 48)
            over_batches(pe, part)

            def project_out(t):
                for h in range(2):
                    if t:
                        pe.wait_ge(res_done, 2 * t - 1 + h)
                    for j in range(J):
                        mm = pe.matmul(stp[0][:, h, 0:BLK], wo[:, j, h * 128:h * 128 + 128],
                                       attn[:, j, t * BLK:t * BLK + BLK], start=(j == 0), stop=(j == J - 1))
                    mm.then_inc(y_ready, 1)

            def turn_x1(t):
                pe.wait_ge(res_done, 2 * (t + 1))
                if t:
                    pe.wait_ge(x1_done, 2 * t)
                for a in range(4):
                    for h in range(2):
                        c0 = t * BLK + a * TM
                        mm = pe.transpose(sbk[a // 2][0:TM, a % 2 * 256 + h * 128:a % 2 * 256 + h * 128 + 128],
                                          resid[:, h, c0:c0 + TM], ident[:, :])
                mm.then_inc(x1t_ready, 1)

            def turn_x2(t):
                pe.wait_ge(x2n_done, 4 * (t + 1))
                if t:
                    pe.wait_ge(x2T_done, 2 * t)
                for a in range(4):
                    for h in range(2):
                        mm = pe.transpose([obk, misc][h][:, a * TM:a * TM + TM],
                                          x1nat[:, 4 * t + a, h * 128:h * 128 + 128], ident[0:TM, 0:TM])
                mm.then_inc(x2t_ready, 1)

            def route(t):
                pe.wait_ge(x2T_done, 2 * (t + 1))
                for a in range(4):
                    for h in range(2):
                        n = 4 * t + a
                        mm = pe.matmul(stp[1][0:TM, 0, n * E:n * E + E], x2T[t % 2][:, h, a * TM:a * TM + TM],
                                       gate[:, h, :], start=(h == 0), stop=(h == 1))
                mm.then_inc(lg_ready, 1)

            def turn_shares(t):
                if t < NBLK - 1:
                    pe.wait_ge(cp_step, 5 * (t + 1))
                else:
                    pe.wait_ge(cp_last, 5)
                for a in range(4):
                    mm = pe.transpose(turned_shares(t)[:, a * TM:a * TM + TM], cparts[:, 4 * t + a, :],
                                      identb[0:TM, 0:TM])
                mm.then_inc(ct_ready, 1)

            pe.wait_ge(norm_step, 4 * B)
            project_out(0)
            project_out(1)
            turn_x1(0)
            project_out(2)
            turn_x1(1)
            turn_x2(0)
            project_out(3)
            turn_x1(2)
            route(0)
            turn_x2(1)
            turn_x1(3)
            route(1)
            turn_x2(2)
            route(2)
            turn_x2(3)
            route(3)
            pe.wait_ge(res_done, 2 * NBLK)
            pe.wait_ge(x1_done, 2 * NBLK)
            for t in range(NBLK):
                turn_shares(t)
            pe.wait_ge(score_done, 2)
            pe.wait_ge(ct_done, NBLK)
            pe.wait_ge(sel_in, 16)
            pe.wait_ge(x2_cut, NBLK)
            def down(s, k):
                pe.wait_ge(hid_step, 4 * s + 4)
                pe.wait_ge(d_cut[1], s + 1)
                for h in range(2):
                    for n, (a, z) in enumerate(PARTS):
                        mm = pe.matmul([obk, misc][h][:, 0:BLK], wdp[k % 2][a][:, h, :], hidp[k % 2][z][:, :],
                                       start=(k == 0 and n == 0), stop=(k == NH - 1 and n == 2))
                mm.then_inc(down_done, 1)

            def tiles(t, first):
                for k in range(NH):
                    s = NH * t + k
                    if not (first and k < 2):
                        pe.wait_ge(hid_step, 4 * (s - 2) + 2)
                    pe.wait_ge(gu_cut[1], s + 1)
                    for o in range(2):
                        for h in range(2):
                            for n, (a, z) in enumerate(PARTS):
                                pe.matmul(stp[k % 2][:, o, 0:BLK], wgup[k % 2][a][:, 2 * o + h, :],
                                          x2p[z][:, h, bass.ds(t * BLK, BLK)],
                                          start=(h == 0 and n == 0), stop=(h == 1 and n == 2))
                    pe.matmul(sbk[k % 2][:, 0:BLK], sel[:, k * 128:k * 128 + 128], combine[:, bass.ds(t * BLK, BLK)],
                              start=True, stop=True).then_inc(gu_ready, 1)
                    if k == 2 and not first:
                        pe.wait_ge(out_done, t)
                    if not (first and k < 2):
                        down(s - 2, (k - 2) % NH)

            tiles(0, True)
            with pe.Fori(1, NBLK) as t:
                tiles(t, False)
            for k in (NH - 2, NH - 1):
                down(NH * (NBLK - 1) + k, k)

        @block.scalar
        def _(act):
            act.wait_ge(ones_set, 1)
            for n in range(CREDIT):
                nc.scalar.activation(warm[:, n:n + 1], warm[:, n:n + 1], ACT.Exp).then_inc(exp_done, 1)
            def take_v(b, p, t):
                act.wait_ge(vt_ready, 3 * b + t + 1)
                for a, z, ks in ([(0, 4, 128)] if t < 2 else [(0, 3, 128), (3, 4, CHUNK[-1][1])]):
                    nc.scalar.copy(vaug[p][0:ks, 4 * t + a:4 * t + z, :, 0:DH],
                                          misc[0:ks, :].rearrange("k (c w g d) -> k c w g d", w=2, g=G, d=DH)
                                          [:, a:z, 1]).then_inc(v_done, 1)

            def part(b, i, p, now=False, nxt=False, turn=False, kv=False, end=False):
                for w in included(now, nxt, turn, kv, end):
                    if w[0] == "st":
                        c = w[1]
                        ks = CHUNK[c][1]
                        act.wait_ge(st_ready, NC * b + c + 1)
                        nc.scalar.activation(probs[c % 2][0:ks, :].rearrange("k (a n) -> k a n", a=2),
                                             stp[c % 2][0:ks, :, 0:448], ACT.Exp).then_inc(exp_done, 1)
                    elif w[0] == "vt" and w[1] == 2:
                        take_v(b + 1, (p + 1) % 2, 2)
                    elif w[0] == "vt":
                        take_v(b + 2, p, w[1])
                    elif w[0] == "kv" and w[2] == 1:
                        t = w[1]
                        k = 3 * (b + 2) + t
                        n = (p + t) % 2
                        ts = THIRD[t][1]
                        act.wait_ge(kv_ready, k + 1)
                        if not isinstance(k, int) or k >= 2:
                            act.wait_ge(vt_ready, k - 1)
                            act.wait_ge(k_cut, 3 * (k - 1))
                            act.wait_ge(kw_done, 32 * (k - 1))
                        nc.scalar.copy(kparts[n][:, 0, 0:ts], misc[0:64, 0:ts]).then_inc(kv_out, 1)
                        nc.scalar.copy(kvf[n][:, 0:ts], misc[:, 0:ts]).then_inc(kv_out, 1)
                    elif w[0] == "cx":
                        k, src, dst, ks, load = after(b, i, p, w[1])
                        if load:
                            act.wait_ge(*load)
                        if not isinstance(k, int) or k >= 2:
                            act.wait_ge(kv_ready, k - 1)
                        nc.scalar.copy(dst[0][:, :, 0:ks], src).then_inc(cx_cut[0], 1)

            act.wait_ge(wkv_in, 32)
            nc.scalar.copy(wkvp[0][:, :, :], wkv[:, :, :]).then_inc(wkv_cut[0], 1)
            act.wait_ge(kvin_in[0], 16)
            nc.scalar.copy(cxp[0][0][:, :, :], kvin[0][:, :, 0:512]).then_inc(cx_cut[0], 1)
            act.wait_ge(var_done, 1)
            nc.scalar.activation(std[:, 0:NT], var[:, 0:NT], ACT.Sqrt).then_inc(std_done, 1)
            act.wait_ge(ones_set, 4)
            first_batch(part)

            for n in range(NT // 2):
                act.wait_ge(xt_ready, n + 1)
                nc.scalar.copy(xnT[:, :, n * 256:n * 256 + 256],
                               sbk[n % 2][:, :].rearrange("p (h t) -> p h t", h=2)).then_inc(xt_done, 1)
            for k in range(2 * NBLK):
                m, t = divmod(k, NBLK)
                act.wait_ge(q_ready, k + 1)
                nc.scalar.mul(qparts[m][:, 0, t * BLK:t * BLK + BLK], qbank[t][:, 0:BLK], DH ** -0.5) \
                    .then_inc(q_out, 1)
                if k >= 2:
                    act.wait_ge(q_cut, 3 * (k - 1))
                nc.scalar.mul(qf[k % 2][:, :], qbank[t][:, 0:BLK], DH ** -0.5).then_inc(q_out, 1)

            over_batches(act, part)

            def take_x1(t):
                act.wait_ge(x1t_ready, t + 1)
                for a in range(2):
                    nc.scalar.copy(x1nat[:, 4 * t + 2 * a:4 * t + 2 * a + 2, :],
                                   sbk[a][0:TM, :].rearrange("p (a d) -> p a d", a=2)).then_inc(x1_done, 1)

            def root(t):
                c = slice(4 * t, 4 * t + 4)
                act.wait_ge(var_done, t + 2)
                nc.scalar.activation(std[0:TM, c], var[0:TM, c], ACT.Sqrt).then_inc(std_done, 1)

            def take_x2(t):
                act.wait_ge(x2t_ready, t + 1)
                if t >= 2:
                    act.wait_ge(lg_ready, t - 1)
                    act.wait_ge(x2_cut, t - 1)
                for h in range(2):
                    nc.scalar.copy(x2T[t % 2][:, h, :], [obk, misc][h][:, 0:BLK]).then_inc(x2T_done, 1)
                act.wait_ge(x2T_done, 2 * (t + 1))
                for h in range(2):
                    nc.scalar.copy(x2p[0][:, h, t * BLK:t * BLK + BLK], x2T[t % 2][:, h, :]).then_inc(x2_high, 1)

            def take_scores(t, z):
                act.wait_ge(lg_ready, z)
                nc.scalar.activation(score[:, 4 * t:4 * z, 0:E],
                                     stp[1][0:TM, 0, 4 * t * E:4 * z * E].rearrange("p (n e) -> p n e", e=E),
                                     ACT.Sigmoid).then_inc(score_done, 1)

            def take_shares(t):
                act.wait_ge(ct_ready, t + 1)
                nc.scalar.copy(combine[0:3 * E, t * BLK:t * BLK + BLK], turned_shares(t)).then_inc(ct_done, 1)

            def cut_gu(k):
                nc.scalar.copy(wgup[k % 2][0][:, :, :], wmoe[:, k, 0:4, :]).then_inc(gu_cut[0], 1)

            def cut_d(k):
                nc.scalar.copy(wdp[k % 2][0][:, :, :], wmoe[:, k, 4:6, :]).then_inc(d_cut[0], 1)

            take_x1(0)
            root(0)
            take_x1(1)
            root(1)
            take_x2(0)
            take_x1(2)
            root(2)
            take_x2(1)
            take_x1(3)
            root(3)
            wait_weights(act, 0)
            cut_gu(0)
            cut_gu(1)
            take_x2(2)
            take_scores(0, NBLK - 1)
            take_x2(3)
            take_scores(NBLK - 1, NBLK)
            for t in range(NBLK):
                take_shares(t)

            def tiles(t, first):
                for k in range(NH):
                    act.wait_ge(gu_ready, NH * t + k + 1)
                    nc.scalar.activation(silu[k % 2][:, :], stp[k % 2][:, 0, 0:BLK], ACT.Silu).then_inc(silu_done, 1)
                    if first:
                        wait_weights(act, k + 2)
                    cut_gu((k + 2) % NH)
                    if not (first and k == 0):
                        cut_d((k - 1) % NH)

            tiles(0, True)
            with act.Fori(1, NBLK) as t:
                tiles(t, False)
            act.wait_ge(down_done, NH * NBLK - 2)
            cut_d(NH - 1)

        @block.gpsimd
        def _(pool):
            nc.gpsimd.memset(warm[:, :], 0.0).then_inc(ones_set, 1)
            nc.gpsimd.memset(alive[:, :], 1.0).then_inc(ones_set, 1)
            for n in range(2):
                nc.gpsimd.memset(vaug[n][:, :, :, DH:32], 1.0).then_inc(ones_set, 1)

            def take_q(b, p):
                nc.gpsimd.tensor_tensor(qs[p][:, :].rearrange("r (h q) -> r h q", h=H), qst[:, :, bass.ds(b * NQ, NQ)],
                                        alive[:, bass.ds(b, 1)].unsqueeze(2).to_broadcast([ROWS, H, NQ]), ALU.mult) \
                    .then_inc(qs_done, 1)

            def part(b, i, p, now=False, nxt=False, turn=False, kv=False, end=False):
                for t in range(3 if kv else 0):
                    k, src, dst, ks, _ = after(b, i, p, t)
                    pool.wait_ge(cx_cut[0], k + 1)
                    nc.gpsimd.tensor_tensor(dst[1][:, :, 0:ks], src, dst[0][:, :, 0:ks], ALU.subtract) \
                        .then_inc(cx_cut[1], 1)
                    if turn and not now and t == 2:
                        pool.wait_ge(ones_set, 4)
                        pool.wait_ge(rows_in, 48)
                        pool.wait_ge(alive_in, 16)
                        pool.wait_ge(qst_in, 16 * 2 * NBAND)
                        take_q(0, 0)
                        take_q(1, 1)
                    k = 3 * (b + 2) + t
                    n = (p + t) % 2
                    ts = THIRD[t][1]
                    pool.wait_ge(kv_out, 2 * k + 2)
                    if not (isinstance(k, int) and k == 0):
                        pool.wait_ge(k_cut, 3 * k)
                    nc.gpsimd.tensor_tensor(kres[:, 0:ts], kvf[n][0:64, 0:ts], kparts[n][:, 0, 0:ts],
                                            ALU.subtract).then_inc(k_cut, 1)
                    nc.gpsimd.tensor_tensor(kparts[n][:, 1, 0:ts], kvf[n][0:64, 0:ts], kparts[n][:, 0, 0:ts],
                                            ALU.subtract).then_inc(k_cut, 1)
                    pool.wait_ge(k_cut, 3 * k + 2)
                    nc.gpsimd.tensor_tensor(kparts[n][:, 2, 0:ts], kres[:, 0:ts], kparts[n][:, 1, 0:ts],
                                            ALU.subtract).then_inc(k_cut, 1)
                    if now and t == 1:
                        pool.wait_ge(st_ready, NC * b + 1)
                        pool.wait_ge(qb_done, b + 1)
                        take_q(b + 2, p)

            pool.wait_ge(wkv_cut[0], 1)
            nc.gpsimd.tensor_tensor(wkvp[1][:, :, :], wkv[:, :, :], wkvp[0][:, :, :], ALU.subtract) \
                .then_inc(wkv_cut[1], 1)
            pool.wait_ge(cx_cut[0], 1)
            nc.gpsimd.tensor_tensor(cxp[0][1][:, :, :], kvin[0][:, :, 0:512], cxp[0][0][:, :, :], ALU.subtract) \
                .then_inc(cx_cut[1], 1)
            first_batch(part)
            over_batches(pool, part)

            def cut_x2(t):
                c = slice(t * BLK, t * BLK + BLK)
                pool.wait_ge(x2_high, 2 * (t + 1))
                nc.gpsimd.tensor_tensor(x2p[1][:, :, c], x2T[t % 2][:, :, :], x2p[0][:, :, c], ALU.subtract) \
                    .then_inc(x2_cut, 1)

            def cut_shares(t):
                n = slice(4 * t, 4 * t + 4)
                w = wrec[:, n].unsqueeze(2).to_broadcast([TM, 4, E])
                pool.wait_ge(chosen_done, t + 1)
                nc.gpsimd.tensor_tensor(share[:, n], chosen[:, n], w, ALU.mult).then_inc(cp_step, 1)
                pool.wait_ge(cp_step, 5 * t + 1)
                nc.gpsimd.tensor_copy(cparts[:, n, 0:E], share[:, n]).then_inc(cp_step, 1)
                pool.wait_ge(cp_step, 5 * t + 2)
                nc.gpsimd.tensor_tensor(cres[:, n], share[:, n], cparts[:, n, 0:E], ALU.subtract).then_inc(cp_step, 1)
                pool.wait_ge(cp_step, 5 * t + 3)
                nc.gpsimd.tensor_copy(cparts[:, n, E:2 * E], cres[:, n]).then_inc(cp_step, 1)
                pool.wait_ge(cp_step, 5 * t + 4)
                nc.gpsimd.tensor_tensor(cparts[:, n, 2 * E:3 * E], cres[:, n], cparts[:, n, E:2 * E], ALU.subtract) \
                    .then_inc(cp_step, 1)

            def cut_gu(s, k):
                pool.wait_ge(gu_cut[0], s + 1)
                nc.gpsimd.tensor_tensor(wgup[k % 2][1][:, :, :], wmoe[:, k, 0:4, :], wgup[k % 2][0][:, :, :],
                                        ALU.subtract).then_inc(gu_cut[1], 1)

            def cut_d(s, k):
                pool.wait_ge(d_cut[0], s + 1)
                nc.gpsimd.tensor_tensor(wdp[k % 2][1][:, :, :], wmoe[:, k, 4:6, :], wdp[k % 2][0][:, :, :],
                                        ALU.subtract).then_inc(d_cut[1], 1)

            cut_x2(0)
            cut_x2(1)
            wait_weights(pool, 0)
            cut_gu(0, 0)
            cut_gu(1, 1)
            cut_x2(2)
            cut_shares(0)
            cut_x2(3)
            for t in range(1, NBLK - 1):
                cut_shares(t)

            def tiles(t, first):
                for k in range(NH):
                    s = NH * t + k
                    if first:
                        wait_weights(pool, k + 2)
                    cut_gu(s + 2, (k + 2) % NH)
                    if not (first and k == 0):
                        cut_d(s - 1, (k - 1) % NH)

            tiles(0, True)
            with pool.Fori(1, NBLK) as t:
                tiles(t, False)
            cut_d(NH * NBLK - 1, NH - 1)

        @block.vector
        def _(dve):
            step = [0]

            def own(ins):
                ins.then_inc(vec, 1)
                step[0] += 1
                return step[0]

            dve.wait_ge(mask_in, 16)
            nc.vector.tensor_scalar(maskb, maskin, -1.0, -MASKED, ALU.add, ALU.mult) \
                .then_inc(mask_cut, 1)
            dve.wait_ge(mask_cut, 1)
            nc.vector.tensor_reduce(some[:, :], maskb, AX_X, ALU.max).then_inc(mask_cut, 1)
            dve.wait_ge(mask_cut, 2)
            nc.vector.tensor_scalar(some[:, :], some[:, :], -1.0, None, ALU.is_ge).then_inc(mask_cut, 1)

            def layer_norm(x, rows, tiles, turn, done):
                c = slice(tiles[0], tiles[-1] + 1)
                r = slice(0, rows)
                for n in tiles:
                    last = own(nc.vector.bn_stats(stats[r, n, :], x[:, n, :]))
                dve.wait_ge(vec, last)
                for n in tiles:
                    last = own(nc.vector.bn_aggr(mv[r, n, :], stats[r, n, :]))
                dve.wait_ge(vec, last)
                nc.vector.tensor_scalar(var[r, c], mv[r, c, 1], EPS, None, ALU.add).then_inc(var_done, 1)
                dve.wait_ge(std_done, turn)
                dve.wait_ge(vec, own(nc.vector.reciprocal(rstd[r, c], std[r, c])))
                dve.wait_ge(vec, own(nc.vector.tensor_tensor(newt[r, c], rstd[r, c], rstd[r, c], ALU.mult)))
                dve.wait_ge(vec, own(nc.vector.tensor_tensor(newt[r, c], newt[r, c], var[r, c], ALU.mult)))
                dve.wait_ge(vec, own(nc.vector.tensor_scalar(newt[r, c], newt[r, c], -0.5, 1.5, ALU.mult, ALU.add)))
                dve.wait_ge(vec, own(nc.vector.tensor_tensor(rstd[r, c], rstd[r, c], newt[r, c], ALU.mult)))
                for n in tiles:
                    nc.vector.tensor_scalar(x[:, n, :], x[:, n, :], mv[r, n, 0:1], rstd[r, n:n + 1],
                                            ALU.subtract, ALU.mult).then_inc(done, 1)

            dve.wait_ge(x_in, 16)
            layer_norm(xnat, 128, range(NT), 1, xn_done)
            for k in range(2 * NBLK):
                m, t = divmod(k, NBLK)
                q = qparts[m][:, :, t * BLK:t * BLK + BLK]
                dve.wait_ge(q_out, 2 * (k + 1))
                nc.vector.tensor_tensor(qres[:, :], qf[k % 2][:, :], q[:, 0], ALU.subtract).then_inc(q_cut, 1)
                dve.wait_ge(q_cut, 3 * k + 1)
                nc.vector.tensor_copy(q[:, 1], qres[:, :]).then_inc(q_cut, 1)
                dve.wait_ge(q_cut, 3 * k + 2)
                nc.vector.tensor_tensor(q[:, 2], qres[:, :], q[:, 1], ALU.subtract).then_inc(q_cut, 1)
                dve.wait_ge(q_cut, 3 * k + 3)
            nc.vector.memset(nmax[:, :], 0.0).then_inc(o_done, 1)
            dve.wait_ge(o_done, 1)

            def minus_max(b, p):
                dve.wait_ge(max_done, NU * (b + 1))
                nc.vector.tensor_reduce(nmax[:, :], maxp[:, :, :], AX_X, ALU.max, negate=True) \
                    .then_inc(nmax_step, 1)
                dve.wait_ge(nmax_step, 5 * b + 1)
                nc.vector.tensor_copy(nparts[:, :, 0], nmax[:, :]).then_inc(nmax_step, 1)
                dve.wait_ge(nmax_step, 5 * b + 2)
                nc.vector.tensor_tensor(nres[:, :], nmax[:, :], nparts[:, :, 0], ALU.subtract) \
                    .then_inc(nmax_step, 1)
                dve.wait_ge(nmax_step, 5 * b + 3)
                nc.vector.tensor_copy(nparts[:, :, 1], nres[:, :]).then_inc(nmax_step, 1)
                dve.wait_ge(nmax_step, 5 * b + 4)
                nc.vector.tensor_tensor(nparts[:, :, 2], nres[:, :], nparts[:, :, 1], ALU.subtract) \
                    .then_inc(nmax_step, 1)
                dve.wait_ge(nmaxT_ready, b + 1)
                dve.wait_ge(qb_done, b + 1)
                nc.vector.tensor_copy(qb[p][EXTRA:EXTRA + 3, :], sbkb[EXTRA:EXTRA + 3, 0:QH]) \
                    .then_inc(qmax_done, 1)

            def finish(b, n):
                if n == 0:
                    dve.wait_ge(pv_ready, b + 1)
                    nc.vector.tensor_copy(attn[:, :, bass.ds(b * NQ, NQ)],
                                          obk[:, 0:224].rearrange("p (j q) -> p j q", j=J)).then_inc(norm_step, 1)
                    nc.vector.stream_shuffle(ssum, obk[:, 0:224], UP).then_inc(o_done, 1)
                elif n < 3:
                    if n == 1:
                        dve.wait_ge(o_done, b + 2)
                    c = slice((n - 1) * 112, n * 112)
                    nc.vector.reciprocal(srec[:, c], ssum[:, c]).then_inc(norm_step, 1)
                else:
                    o = attn[:, :, bass.ds(b * NQ, NQ)]
                    dve.wait_ge(norm_step, 4 * b + 3)
                    nc.vector.tensor_tensor(o, o, srec.rearrange("p (j q) -> p j q", j=J), ALU.mult) \
                        .then_inc(norm_step, 1)

            def part(b, i, p, now=False, nxt=False, turn=False, kv=False, end=False):
                bn = b + 1
                for w in included(now, nxt, turn, kv, end):
                    if w[0] == "u":
                        t, q = divmod(w[1], 2 * G)
                        dve.wait_ge(s_ready, NU * bn + w[1] + 1)
                        nc.vector.tensor_reduce(maxp[:, q, t:t + 1], sbk[w[1] % 2][0:TQ, 0:THIRD[t][1]], AX_X,
                                                ALU.max).then_inc(max_done, 1)
                    elif w[0] == "qb":
                        dve.wait_ge(qs_done, bn + 1)
                        if now:
                            dve.wait_ge(st_ready, NC * b + 1)
                        nc.vector.tensor_copy(qb[(p + 1) % 2][:, :], qs[(p + 1) % 2][:, :]).then_inc(qb_done, 1)
                    elif w[0] == "mx":
                        minus_max(bn, (p + 1) % 2)
                    elif w[0] == "o":
                        finish(b - 1, w[1])

            over_batches(dve, part)

            dve.wait_ge(resid_in, 16)
            own(nc.vector.memset(combine[3 * E:3 * E + 1, :], 1.0))
            dve.wait_ge(vec, own(nc.vector.memset(score[:, :, E:E + 2], 2.0)))

            def add_attention(t):
                for h in range(2):
                    dve.wait_ge(y_ready, 2 * t + h + 1)
                    r = resid[:, h, t * BLK:t * BLK + BLK]
                    nc.vector.tensor_tensor(r, r, stp[0][:, h, 0:BLK], ALU.add).then_inc(res_done, 1)

            def norm(t):
                dve.wait_ge(x1_done, 2 * (t + 1))
                layer_norm(x1nat, TM, range(4 * t, 4 * t + 4), t + 2, x2n_done)

            def choose(t):
                c = slice(4 * t, 4 * t + 4)
                dve.wait_ge(score_done, 1 if t < NBLK - 1 else 2)
                for n in range(4 * t, 4 * t + 4):
                    last = own(nc.vector.max(top8[:, n, :], score[:, n, :]))
                dve.wait_ge(vec, last)
                total = own(nc.vector.tensor_reduce(wsum[:, c], top8[:, c, 2:8], AX_X, ALU.add))
                for n in range(4 * t, 4 * t + 4):
                    last = own(nc.vector.match_replace(rest[:, n, :], top8[:, n, :], score[:, n, :], -1.0))
                dve.wait_ge(vec, total)
                total = own(nc.vector.tensor_scalar(wsum[:, c], wsum[:, c], 1e-20, None, ALU.add))
                dve.wait_ge(vec, total)
                total = own(nc.vector.reciprocal(wrec[:, c], wsum[:, c]))
                dve.wait_ge(vec, total)
                nc.vector.scalar_tensor_tensor(out=chosen[:, c, :], in0=rest[:, c, 0:E], scalar=0.0,
                                               in1=score[:, c, 0:E], op0=ALU.is_lt, op1=ALU.mult) \
                    .then_inc(chosen_done, 1)

            add_attention(0)
            add_attention(1)
            norm(0)
            add_attention(2)
            norm(1)
            add_attention(3)
            norm(2)
            norm(3)
            for t in range(NBLK):
                choose(t)
            n = slice(4 * (NBLK - 1), NM)
            w = wrec[:, n].unsqueeze(2).to_broadcast([TM, 4, E])
            dve.wait_ge(chosen_done, NBLK)
            nc.vector.tensor_tensor(share[:, n], chosen[:, n], w, ALU.mult).then_inc(cp_last, 1)
            dve.wait_ge(cp_last, 1)
            nc.vector.tensor_copy(cparts[:, n, 0:E], share[:, n]).then_inc(cp_last, 1)
            dve.wait_ge(cp_last, 2)
            nc.vector.tensor_tensor(cres[:, n], share[:, n], cparts[:, n, 0:E], ALU.subtract).then_inc(cp_last, 1)
            dve.wait_ge(cp_last, 3)
            nc.vector.tensor_copy(cparts[:, n, E:2 * E], cres[:, n]).then_inc(cp_last, 1)
            dve.wait_ge(cp_last, 4)
            nc.vector.tensor_tensor(cparts[:, n, 2 * E:3 * E], cres[:, n], cparts[:, n, E:2 * E], ALU.subtract) \
                .then_inc(cp_last, 1)

            def output(t):
                dve.wait_ge(down_done, NH * (t + 1))
                for h in range(2):
                    r = resid[:, h, bass.ds(t * BLK, BLK)]
                    ins = nc.vector.tensor_tensor(r, r, [obk, misc][h][:, 0:BLK], ALU.add)
                    if h == 0:
                        ins.then_inc(vec, 1)
                ins.then_inc(out_done, 1)

            def tiles(t, first):
                for k in range(NH):
                    s = NH * t + k
                    dve.wait_ge(silu_done, s + 1)
                    nc.vector.tensor_tensor(gated[:, :], silu[k % 2][:, :], stp[k % 2][:, 1, 0:BLK],
                                            ALU.mult).then_inc(hid_step, 1)
                    dve.wait_ge(hid_step, 4 * s + 1)
                    nc.vector.tensor_tensor(hid[:, :], gated[:, :], sbk[k % 2][:, 0:BLK], ALU.mult) \
                        .then_inc(hid_step, 1)
                    if not (first and k < 2):
                        dve.wait_ge(down_done, s - 1)
                    dve.wait_ge(hid_step, 4 * s + 2)
                    nc.vector.tensor_copy(hidp[k % 2][0][:, :], hid[:, :]).then_inc(hid_step, 1)
                    dve.wait_ge(hid_step, 4 * s + 3)
                    nc.vector.tensor_tensor(hidp[k % 2][1][:, :], hid[:, :], hidp[k % 2][0][:, :],
                                            ALU.subtract).then_inc(hid_step, 1)
                    if k == 1 and not first:
                        output(t - 1)

            tiles(0, True)
            with dve.Fori(1, NBLK) as t:
                tiles(t, False)
            output(NBLK - 1)


NP_BF16 = np.dtype(mybir.dt.np(BF16))


def _bf16_parts(a):
    a = np.asarray(a, np.float64)
    parts = []
    for _ in range(3):
        h = a.astype(NP_BF16)
        parts.append(h)
        a = a - h.astype(np.float64)
    return parts


def _constants():
    bf = NP_BF16
    slope = (np.float32(2.0 ** (-8.0 / H)) ** np.arange(1, H + 1, dtype=np.float32)).astype(np.float32)
    slope_parts = _bf16_parts(slope)
    q = np.arange(NQ, dtype=np.float64)
    shift_parts = _bf16_parts(-(slope.astype(np.float64)[:, None] * q[None, :]))
    qrows = np.zeros((ROWS - EXTRA, H, B, NQ), bf)
    for n in range(3):
        qrows[3 + n] = shift_parts[n][:, None, :]
        qrows[6 + n] = slope_parts[n][:, None, None]
        qrows[9 + n] = slope_parts[n][:, None, None]
    qrows[12] = 1.0
    keys = np.arange(NK)
    krows = np.zeros((12, G, NK), bf)
    krows[0:6] = 1.0
    krows[6:9] = (keys // 8 * 8).astype(np.float32)
    krows[9:12] = (keys % 8).astype(np.float32)
    sel = np.zeros((3 * E + 1, HP), bf)
    for e in range(E):
        for n in range(3):
            sel[n * E + e, e * FE:(e + 1) * FE] = 1.0
    sel[3 * E, E * FE:HID] = 1.0
    return {"c_ident": np.eye(128, dtype=np.float32), "c_identb": np.eye(128, dtype=np.float32).astype(bf),
            "c_krows": krows, "c_qrows": qrows.reshape(ROWS - EXTRA, H, T), "c_sel": sel}


def kernel(x, ctx_2048, mask_BxS2_bf1, L0_xattn_Wq, L0_xattn_Wk, L0_xattn_Wv, L0_xattn_Wo, L0_ffn_gate_w,
           L0_ffn_wg, L0_ffn_wu, L0_ffn_wd, L0_ffn_sg, L0_ffn_su, L0_ffn_sd):
    import concourse.bacc as bacc
    from concourse.bass_utils import run_bass_kernel_spmd

    def f(a):
        return np.asarray(a)

    def wide(routed, shared):
        a = np.concatenate([f(routed).transpose(1, 0, 2).reshape(D, E * FE), f(shared)], 1)
        return np.pad(a, ((0, 0), (0, HP - HID)))

    x2 = f(x).reshape(T, D)
    wq = f(L0_xattn_Wq).reshape(D, 2, 8, DH).transpose(0, 1, 3, 2).reshape(D, D)
    wk = f(L0_xattn_Wk).reshape(D, G, DH).transpose(0, 2, 1).reshape(D, G * DH)
    wo = np.pad(f(L0_xattn_Wo).reshape(G, J, DH, D).transpose(0, 2, 1, 3), ((0, 0), (0, DH), (0, 0), (0, 0)))
    gate_up = np.stack([wide(L0_ffn_wg, L0_ffn_sg), wide(L0_ffn_wu, L0_ffn_su)])
    down = np.pad(np.concatenate([f(L0_ffn_wd).reshape(E * FE, D), f(L0_ffn_sd)], 0), ((0, HP - HID), (0, 0)))
    arrays = {
        "x_nat": x2,
        "x_tr": x2.T,
        "ctx_tr": np.pad(f(ctx_2048).transpose(0, 2, 1), ((0, 1), (0, 0), (0, 0))),
        "mask": f(mask_BxS2_bf1).view(np.uint8),
        "w_q": wq,
        "w_kv": np.concatenate([wk, f(L0_xattn_Wv)], 1),
        "w_o": wo.reshape(128, J, D),
        "gate_w": f(L0_ffn_gate_w),
        "w_moe": np.stack([*gate_up.reshape(4, 128, NH, 128), *down.reshape(NH, 128, 2, 128).transpose(2, 1, 0, 3)],
                          2),
        **_constants(),
    }
    arrays = {n: np.ascontiguousarray(a) for n, a in arrays.items()}
    nc = bacc.Bacc("TRN2", target_bir_lowering=False, num_devices=1)
    aps = [_dram_in(nc, n, a.shape, mybir.dt.from_np(a.dtype)) for n, a in arrays.items()]
    out = nc.dram_tensor("out_tr", (D, T), F32, kind="ExternalOutput").ap()
    build(nc, *aps, out)
    r = run_bass_kernel_spmd(nc, [arrays], core_ids=[0])
    return np.ascontiguousarray(r.results[0]["out_tr"].T).reshape(B, NQ, D)
```
